# Optimizing a Trainium2 kernel written in Bass

```python
import numpy as np
import jax
import jax.numpy as jnp

def _softmax(x, axis=-1):
    return jax.nn.softmax(x, axis=axis)

def _gelu(x):
    return jax.nn.gelu(x, approximate=True)

def _silu(x):
    return jax.nn.silu(x)

def _sigmoid(x):
    return jax.nn.sigmoid(x)

def _layernorm(x, axis=-1, eps=1e-05):
    m = jnp.mean(x, axis=axis, keepdims=True)
    v = jnp.var(x, axis=axis, keepdims=True)
    return (x - m) / jnp.sqrt(v + eps)

def _scatter_add(tgt, idx, src, axis=0):
    return tgt.at[idx].add(src)

def _segment_sum(src, seg, n):
    return jax.ops.segment_sum(src, seg, n)
kernel_name = 'mk_adaln_d1_jaxref_r4_ef538e'

def setup_inputs(seed: int=0):
    np.random.seed(seed)
    _w = jnp.asarray

    def _L0_attn_setup():
        import jax, jax.numpy as jnp
        import numpy as np
        B, S, HID = (4, 1024, 512)
        H, NB = (16, 4)
        D = HID // H
        EPS = 1e-06

        def elu_plus_one(x):
            return jax.nn.elu(x) + 1.0

        def _reference_tuple_inner(hidden_states, Wq, Wk, Wv, Wo, bank_weights, memories, memory_norms):
            b, s, _ = hidden_states.shape

            def proj(W):
                return (hidden_states @ W.T).reshape(b, s, H, D).transpose(0, 2, 1, 3)
            q, k, v = (proj(Wq), proj(Wk), proj(Wv))
            sigma_q = elu_plus_one(q)
            a_unnorm = jnp.einsum('bhsd,nhde->nbhse', sigma_q, memories)
            norm = jnp.einsum('bhsd,nhd->nbhs', sigma_q, memory_norms)
            a = a_unnorm / jnp.clip(norm, EPS, None)[..., None]
            active = (memory_norms.sum(axis=(1, 2)) >= EPS).astype(a.dtype)
            a = a * active[:, None, None, None, None]
            weights = jax.nn.softmax(bank_weights, axis=-1)
            combined = jnp.einsum('nbhse,hn->bhse', a, weights)
            sigma_k = elu_plus_one(k)
            mem0, norm0 = (memories[0], memory_norms[0])
            retr = jnp.einsum('bhsd,hde->bhse', sigma_k, mem0)
            knorm = jnp.clip(jnp.einsum('bhsd,hd->bhs', sigma_k, norm0), EPS, None)
            delta_v = v - retr / knorm[..., None]
            mem_update = jnp.einsum('bhsd,bhse->hde', sigma_k, delta_v) / (b * s)
            new_mem0 = jax.lax.stop_gradient(mem0 + mem_update)
            new_norm0 = jax.lax.stop_gradient(norm0 + sigma_k.sum(axis=(0, 2)) / b)
            out = combined.transpose(0, 2, 1, 3).reshape(b, s, HID) @ Wo.T
            return (out, new_mem0, new_norm0)
        key = jax.random.key(seed)
        ks = jax.random.split(key, 8)
        return {'hidden_states': jax.random.normal(ks[0], (B, S, HID), jnp.float32), 'Wq': jax.random.normal(ks[1], (HID, HID), jnp.float32) * 0.02, 'Wk': jax.random.normal(ks[2], (HID, HID), jnp.float32) * 0.02, 'Wv': jax.random.normal(ks[3], (HID, HID), jnp.float32) * 0.02, 'Wo': jax.random.normal(ks[4], (HID, HID), jnp.float32) * 0.02, 'bank_weights': jax.random.normal(ks[5], (H, NB), jnp.float32) * 0.02, 'memories': jax.random.uniform(ks[6], (NB, H, D, D), jnp.float32), 'memory_norms': jax.random.uniform(ks[7], (NB, H, D), jnp.float32)}
    _L0_attn_in = _L0_attn_setup()

    def _L0_ffn_setup():
        import jax, jax.numpy as jnp
        import numpy as np

        def _sparsify_2to4(h):
            B, S, I = h.shape
            g = h.reshape(B, S, I // 4, 4)
            a = jnp.abs(g)
            _, idx = jax.lax.top_k(a, 2)
            pos = jnp.arange(4)
            mask = (pos == idx[..., 0:1]) | (pos == idx[..., 1:2])
            return (g * mask.astype(g.dtype)).reshape(B, S, I)
        key = jax.random.key(seed)
        k1, k2, k3, k4 = jax.random.split(key, 4)
        B, S, H, I = (4, 512, 512, 2048)
        x = jax.random.normal(k1, (B, S, H), dtype=jnp.float32)
        w_gate = jax.random.normal(k2, (H, I), dtype=jnp.float32) / np.sqrt(H)
        w_up = jax.random.normal(k3, (H, I), dtype=jnp.float32) / np.sqrt(H)
        w_down = jax.random.normal(k4, (I, H), dtype=jnp.float32) / np.sqrt(I)
        return {'x': x, 'w_gate': w_gate, 'w_up': w_up, 'w_down': w_down}
    _L0_ffn_in = _L0_ffn_setup()
    _L0_c = _w((lambda *s: np.random.randn(*s).astype(np.float32) * 0.05)(4, 512))
    _L0_wmod = _w((lambda *s: np.random.randn(*s).astype(np.float32) * 0.05)(512, 6 * 512) * 512 ** (-0.5))
    _d = {'L0_attn_hidden_states': _L0_attn_in['hidden_states'], 'L0_attn_Wq': _L0_attn_in['Wq'], 'L0_attn_Wk': _L0_attn_in['Wk'], 'L0_attn_Wv': _L0_attn_in['Wv'], 'L0_attn_Wo': _L0_attn_in['Wo'], 'L0_attn_bank_weights': _L0_attn_in['bank_weights'], 'L0_attn_memories': _L0_attn_in['memories'], 'L0_attn_memory_norms': _L0_attn_in['memory_norms'], 'L0_ffn_w_gate': _L0_ffn_in['w_gate'], 'L0_ffn_w_up': _L0_ffn_in['w_up'], 'L0_ffn_w_down': _L0_ffn_in['w_down'], 'L0_c': _L0_c, 'L0_wmod': _L0_wmod}
    _x0 = _d['L0_attn_hidden_states']
    _d['L0_attn_hidden_states'] = jax.random.normal(jax.random.fold_in(jax.random.key(seed), 1), (4, 1024, 512), dtype=_x0.dtype)
    del _x0
    return _d

def reference(L0_attn_hidden_states, L0_attn_Wq, L0_attn_Wk, L0_attn_Wv, L0_attn_Wo, L0_attn_bank_weights, L0_attn_memories, L0_attn_memory_norms, L0_ffn_w_gate, L0_ffn_w_up, L0_ffn_w_down, L0_c, L0_wmod):

    def _L0_attn_ref(hidden_states, Wq, Wk, Wv, Wo, bank_weights, memories, memory_norms):
        import jax, jax.numpy as jnp
        import numpy as np
        B, S, HID = (4, 1024, 512)
        H, NB = (16, 4)
        D = HID // H
        EPS = 1e-06

        def elu_plus_one(x):
            return jax.nn.elu(x) + 1.0

        def _reference_tuple_inner(hidden_states, Wq, Wk, Wv, Wo, bank_weights, memories, memory_norms):
            b, s, _ = hidden_states.shape

            def proj(W):
                return (hidden_states @ W.T).reshape(b, s, H, D).transpose(0, 2, 1, 3)
            q, k, v = (proj(Wq), proj(Wk), proj(Wv))
            sigma_q = elu_plus_one(q)
            a_unnorm = jnp.einsum('bhsd,nhde->nbhse', sigma_q, memories)
            norm = jnp.einsum('bhsd,nhd->nbhs', sigma_q, memory_norms)
            a = a_unnorm / jnp.clip(norm, EPS, None)[..., None]
            active = (memory_norms.sum(axis=(1, 2)) >= EPS).astype(a.dtype)
            a = a * active[:, None, None, None, None]
            weights = jax.nn.softmax(bank_weights, axis=-1)
            combined = jnp.einsum('nbhse,hn->bhse', a, weights)
            sigma_k = elu_plus_one(k)
            mem0, norm0 = (memories[0], memory_norms[0])
            retr = jnp.einsum('bhsd,hde->bhse', sigma_k, mem0)
            knorm = jnp.clip(jnp.einsum('bhsd,hd->bhs', sigma_k, norm0), EPS, None)
            delta_v = v - retr / knorm[..., None]
            mem_update = jnp.einsum('bhsd,bhse->hde', sigma_k, delta_v) / (b * s)
            new_mem0 = jax.lax.stop_gradient(mem0 + mem_update)
            new_norm0 = jax.lax.stop_gradient(norm0 + sigma_k.sum(axis=(0, 2)) / b)
            out = combined.transpose(0, 2, 1, 3).reshape(b, s, HID) @ Wo.T
            return (out, new_mem0, new_norm0)
        return _reference_tuple_inner(hidden_states, Wq, Wk, Wv, Wo, bank_weights, memories, memory_norms)[0]

    def _L0_ffn_ref(x, w_gate, w_up, w_down):
        import jax, jax.numpy as jnp
        import numpy as np

        def _sparsify_2to4(h):
            B, S, I = h.shape
            g = h.reshape(B, S, I // 4, 4)
            a = jnp.abs(g)
            _, idx = jax.lax.top_k(a, 2)
            pos = jnp.arange(4)
            mask = (pos == idx[..., 0:1]) | (pos == idx[..., 1:2])
            return (g * mask.astype(g.dtype)).reshape(B, S, I)
        h = jax.nn.silu(jnp.einsum('bsh,hi->bsi', x, w_gate)) * jnp.einsum('bsh,hi->bsi', x, w_up)
        h_sparse = _sparsify_2to4(h)
        return jnp.einsum('bsi,ih->bsh', h_sparse, w_down)
    x = L0_attn_hidden_states
    mod = (_silu(L0_c) @ L0_wmod).reshape(L0_c.shape[0], 6, 1, -1)
    sa, ca, ga, sb, cb, gb = (mod[:, 0], mod[:, 1], mod[:, 2], mod[:, 3], mod[:, 4], mod[:, 5])
    ga = (2 * (ga >= 0) - 1) * jnp.maximum(jnp.abs(ga), 0.25)
    gb = (2 * (gb >= 0) - 1) * jnp.maximum(jnp.abs(gb), 0.25)
    h = _layernorm(x, axis=-1) * (1 + ca) + sa
    x = x + ga * _L0_attn_ref(h, L0_attn_Wq, L0_attn_Wk, L0_attn_Wv, L0_attn_Wo, L0_attn_bank_weights, L0_attn_memories, L0_attn_memory_norms)
    h = _layernorm(x, axis=-1) * (1 + cb) + sb
    x = x + gb * _L0_ffn_ref(h, L0_ffn_w_gate, L0_ffn_w_up, L0_ffn_w_down)
    return x

_drawn_inputs = setup_inputs


def setup_inputs(seed=0):
    import zlib

    import numpy as np

    out = dict(_drawn_inputs(seed))
    spreads = {}
    factors = {'L0_attn_Wq': 31.021,
     'L0_attn_bank_weights': 64.0,
     'L0_attn_memories': 35.007,
     'L0_attn_memory_norms': 22.023}
    for name, (base, spread) in spreads.items():
        noise = np.random.default_rng([zlib.crc32(name.encode()), seed]).standard_normal(out[name].shape)
        drawn = base * np.exp(spread * noise) if base else spread * noise
        out[name] = jnp.asarray(drawn.astype(out[name].dtype))
    for name, factor in factors.items():
        out[name] = (out[name] * factor).astype(out[name].dtype)
    return out
```

```python
from contextlib import ExitStack

import concourse.bass as bass
from concourse import mybir

F32 = mybir.dt.float32
F32R = mybir.dt.float32r
BF16 = mybir.dt.bfloat16
ALU = mybir.AluOpType
ACT = mybir.ActivationFunctionType
AX_X = mybir.AxisListType.X

P = 128
D = 512
T = 512
S = T // P
K = D // P
B = 4
NB = 4
DH = 32
HG = P // DH
J = 4
CH = 512
LN_EPS = 1e-5
NORM_EPS = 1e-6
X_RING = 3
SA, CA, GA, SB, CB, GB = range(6)


def adaln_kernel(nc, x, wqT, woT, bank_w, mem_hd, norm_hd, w_gate, w_up, w_down, cT, wmod, out):
    tokens = x.shape[0]
    NT = tokens // T
    TB = NT // B
    hidden = w_gate.shape[1]
    CHUNKS = hidden // CH
    SLOTS = 2
    PASSES = CHUNKS // SLOTS
    NT2 = NT * PASSES

    x1_dram = nc.dram_tensor("x1_scratch", (tokens, D), F32, kind="Internal").ap()
    acc_dram = nc.dram_tensor("acc_scratch", (tokens, D), F32, kind="Internal").ap()
    h2_dram = nc.dram_tensor("h2T_scratch", (NT, P, K * T), F32, kind="Internal").ap()
    gate_dram = nc.dram_tensor("gates_scratch", (2, B, D), F32, kind="Internal").ap()

    def tiled(dram):
        return dram.rearrange("(t p s) d -> t p s d", p=P, s=S)

    x_t, x1_t, acc_t, out_t = tiled(x), tiled(x1_dram), tiled(acc_dram), tiled(out)

    with ExitStack() as ctx:
        def sem(name):
            return ctx.enter_context(nc.semaphore(name))

        bank = [ctx.enter_context(nc.psum_tensor(f"bank{i}", [P, 512], F32)) for i in range(8)]

        w_gate_hi, w_gate_lo, w_up_hi, w_up_lo, w_down_hi, w_down_lo = [], [], [], [], [], []

        def slot(stack, c):
            for name, kept, shape in (
                ("w_gate_hi", w_gate_hi, [P, K, J, P]), ("w_gate_lo", w_gate_lo, [P, K, J, P]),
                ("w_up_hi", w_up_hi, [P, K, J, P]), ("w_up_lo", w_up_lo, [P, K, J, P]),
                ("w_down_hi", w_down_hi, [P, J, D]), ("w_down_lo", w_down_lo, [P, J, D]),
            ):
                kept.append(stack.enter_context(nc.sbuf_tensor(f"{name}{c}", shape, F32R)))

        with ExitStack() as phase_a:
            def sba(name, shape, dt=F32):
                return phase_a.enter_context(nc.sbuf_tensor(name, shape, dt))

            wmod_sb = sba("wmod_sb", [P, 3, K, D])
            x_ring = sba("x_ring", [P, X_RING, S, D])
            xn1 = sba("xn1", [P, S, D])
            h1_full = sba("h1_full", [P, 2, T])
            h1_hi = sba("h1_hi", [P, K, T], F32R)
            h1_lo = sba("h1_lo", [P, K, T], F32R)
            exp_q = sba("exp_q", [P, 2, T])
            sigma = sba("sigma", [P, K, T])
            sigma_hi = sba("sigma_hi", [P, K, T], F32R)
            sigma_lo = sba("sigma_lo", [P, K, T], F32R)
            banks_r = sba("banks_r", [P, K, NB, P])
            combined = sba("combined", [P, K, P])
            combT_hi = [sba(f"combT_hi{i}", [P, K, P], F32R) for i in range(2)]
            combT_lo = [sba(f"combT_lo{i}", [P, K, P], F32R) for i in range(2)]
            attn_scaled = sba("attn_scaled", [P, D])
            xn2 = sba("xn2", [P, S, D])
            h2_full = sba("h2_full", [P, K, T])
            wq_hi = sba("wq_hi", [P, K, D], F32R)
            wq_lo = sba("wq_lo", [P, K, D], F32R)
            wo_hi = sba("wo_hi", [P, K, D], F32R)
            wo_lo = sba("wo_lo", [P, K, D], F32R)
            mem_hi = sba("mem_hi", [P, K, NB * P], F32R)
            mem_lo = sba("mem_lo", [P, K, NB * P], F32R)
            ga_all = sba("ga_all", [P, B, D])
            ident = sba("ident", [P, P])
            ones = sba("ones", [P, P])
            mem_raw = sba("mem_raw", [P, K, NB, DH])
            norm_raw = sba("norm_raw", [P, K, NB])
            norm_bd = sba("norm_bd", [P, K, NB, HG])
            bank_sb = sba("bank_sb", [P, K * HG, NB])
            bank_red = sba("bank_red", [P, K * HG])
            active_sum = sba("active_sum", [P, NB])
            bank_gate = sba("bank_gate", [P, K, NB, HG])
            inv_norm = sba("inv_norm", [P, 2, K * NB * HG])
            cT_sb = sba("cT_sb", [P, K, B])
            silu_c = sba("silu_c", [P, K, B])
            mods = sba("mods", [P, 4, K, B])
            gates = sba("gates", [B, 2, D])
            ln_raw = sba("ln_raw", [P, 2, S, 6])
            ln_mv = sba("ln_mv", [P, 2, S, 2])
            ln_var = sba("ln_var", [P, 2, S])
            ln_sd = sba("ln_sd", [P, 2, S])
            ln_rstd = sba("ln_rstd", [P, 2, S])
            ln_shift = sba("ln_shift", [P, 2, S])

        phase_b = ctx
        slot(phase_b, 0)

        def sbb(name, shape, dt=F32):
            return phase_b.enter_context(nc.sbuf_tensor(name, shape, dt))

        slot(phase_b, 1)
        silu_g = sbb("silu_g", [P, 2, T])
        h_act = sbb("h_act", [P, SLOTS, J, T])
        h_abs = sbb("h_abs", [P, J, T])
        pair_hi = sbb("pair_hi", [P, 2, T])
        pair_lo = sbb("pair_lo", [P, 2, T])
        first_wins = sbb("first_wins", [P, 2, T], BF16)
        both_of = sbb("both_of", [P, 2, T], BF16)
        one_each = sbb("one_each", [P, 1, T], BF16)
        keep = sbb("keep", [P, J, T], BF16)
        hs_hi = sbb("hs_hi", [P, J, T], F32R)
        hs_lo = sbb("hs_lo", [P, J, T], F32R)
        h2_raw = sbb("h2_raw", [P, K, T])
        h2_hi = sbb("h2_hi", [P, K, T], F32R)
        h2_lo = sbb("h2_lo", [P, K, T], F32R)
        y = sbb("y", [P, S, D])
        gb_row = sbb("gb_row", [P, D])
        ffn_scaled = sbb("ffn_scaled", [P, 2, D])
        w_raw = sbb("w_raw", [P, K * CH])

        small_in, norm_in, wmod1_in, wmod2_in, wmod_gates_in, wq_in, wo_in = map(sem, (
            "small_in", "norm_in", "wmod1_in", "wmod2_in", "wmod_gates_in", "wq_in", "wo_in"))
        x_in = [sem(f"x_in{i}") for i in range(X_RING)]
        gates_out, ga_in, x1_out, h2_out = map(sem, ("gates_out", "ga_in", "x1_out", "h2_out"))
        ident_zero, ident_ready, consts_ready, setup_dve = map(sem, (
            "ident_zero", "ident_ready", "consts_ready", "setup_dve"))
        silu_c_ready, mods_mm, gates_mm, active_mm, mods_ready, gates_ready = map(sem, (
            "silu_c_ready", "mods_mm", "gates_mm", "active_mm", "mods_ready", "gates_ready"))
        bank_shifted, bank_exp, mem_bd_ready, wa_hi, wa_lo, gate_ready = map(sem, (
            "bank_shifted", "bank_exp", "mem_bd_ready", "wa_hi", "wa_lo", "gate_ready"))
        bn1_done, ag1_done, bn2_done, ag2_done = map(sem, ("bn1_done", "ag1_done", "bn2_done", "ag2_done"))
        var_done, sd_done, rstd_done, shift_done = map(sem, ("var_done", "sd_done", "rstd_done", "shift_done"))
        xn1_done, t1_done, h1_full_done, h1_hi_done, h1_lo_done = map(sem, (
            "xn1_done", "t1_done", "h1_full_done", "h1_hi_done", "h1_lo_done"))
        q_done, exp_done, neg_done, sigma_done, sigma_hi_done, sigma_lo_done = map(sem, (
            "q_done", "exp_done", "neg_done", "sigma_done", "sigma_hi_done", "sigma_lo_done"))
        norm_done, clip_done, recip_done, r_done = map(sem, ("norm_done", "clip_done", "recip_done", "r_done"))
        banks_done, banks_r_done, half_sum_done, comb_done = map(sem, (
            "banks_done", "banks_r_done", "half_sum_done", "comb_done"))
        combT_done, combT_hi_done, combT_lo_done = map(sem, ("combT_done", "combT_hi_done", "combT_lo_done"))
        wo_done, attn_scaled_done, x1_done = map(sem, ("wo_done", "attn_scaled_done", "x1_done"))
        xn2_done, t2_done, h2_full_done = map(sem, ("xn2_done", "t2_done", "h2_full_done"))

        w_in = [sem(f"w_in{i}") for i in range(3 * CHUNKS)]
        w_hi_done, w_lo_dve, w_lo_pool = map(sem, ("w_hi_done", "w_lo_dve", "w_lo_pool"))
        h2_in, h2_hi_done, h2_lo_done = map(sem, ("h2_in", "h2_hi_done", "h2_lo_done"))
        gate_done, up_done, silu_done, h_done, abs_done = map(sem, (
            "gate_done", "up_done", "silu_done", "h_done", "abs_done"))
        mask_step, kept_done, hs_hi_done, hs_lo_done, down_done = map(sem, (
            "mask_step", "kept_done", "hs_hi_done", "hs_lo_done", "down_done"))
        y_in, y_scaled, y_done, y_out = map(sem, ("y_in", "y_scaled", "y_done", "y_out"))

        block = ctx.enter_context(nc.Block())

        def w_dram(c, m):
            cols = slice(c * CH, (c + 1) * CH)
            if m == 2:
                return w_down[cols, :].rearrange("(p j) d -> p j d", j=J)
            return (w_gate, w_up)[m].rearrange("(k p) i -> p k i", p=P)[:, :, cols]

        def w_stage(c, m):
            if c == 0:
                return h_abs[:] if m == 2 else h_act[:, m]
            if (c, m) == (1, 1):
                return y[:]
            return w_raw[:].rearrange("p (a b) -> p a b", b=CH)

        def w_split_views(c, m):
            sl = c % SLOTS
            hi, lo = ((w_gate_hi, w_gate_lo), (w_up_hi, w_up_lo), (w_down_hi, w_down_lo))[m]
            raw = w_stage(c, m)
            if m < 2:
                raw = raw.rearrange("q k (p j) -> q k j p", j=J)
            return hi[sl], lo[sl], raw

        WEIGHTS = [(c, m) for c in range(CHUNKS) for m in range(3)]
        SPLITS = [(0, 0), (0, 1), (0, 2), (1, 0), (1, 1), (1, 2),
                  (2, 0), (2, 1), (3, 0), (3, 1), (2, 2), (3, 2)]
        RANK = {cm: i for i, cm in enumerate(SPLITS)}

        def w_lo_wait(eng, cm):
            if cm[0] == 0:
                eng.wait_ge(w_lo_dve, RANK[cm] + 1)
            else:
                eng.wait_ge(w_lo_pool, RANK[cm] - 2)

        @block.sync
        def _(sp):
            with nc.allow_non_contiguous_dma(reason="16-byte rows of small tables"):
                sp.dma_start(cT_sb[:], cT.rearrange("(k p) b -> p k b", p=P)).then_inc(small_in, 16)
                wmod_k = wmod.rearrange("(k p) (i n) -> p i k n", p=P, n=D)
                for i, block_ in enumerate((SA, CA)):
                    sp.dma_start(wmod_sb[:, i], wmod_k[:, block_]).then_inc(wmod1_in, 16)
                sp.dma_start(x_ring[:, 0], x_t[0]).then_inc(x_in[0], 16)
                sp.dma_start(banks_r[:].rearrange("p a b c -> p a (b c)"),
                             wqT.rearrange("(k p) n -> p k n", p=P)).then_inc(wq_in, 16)
                sp.dma_start(norm_raw[:], norm_hd.rearrange("(k p) n -> p k n", p=P)).then_inc(norm_in, 16)
                sp.dma_start(mem_raw[:], mem_hd.rearrange("(k p) n e -> p k n e", p=P)).then_inc(norm_in, 16)
                sp.dma_start(bank_sb[:], bank_w.partition_broadcast(P)).then_inc(norm_in, 16)
                sp.dma_start(h2_full[:], woT.rearrange("(k p) n -> p k n", p=P)).then_inc(wo_in, 16)
                sp.dma_start(x_ring[:, 2], wmod_k[:, GA]).then_inc(wmod_gates_in, 16)
                sp.dma_start(wmod_sb[:, 2], wmod_k[:, GB]).then_inc(wmod_gates_in, 16)
                sp.dma_start(x_ring[:, 1], x_t[1]).then_inc(x_in[1], 16)
                sp.wait_ge(mods_mm, 1)
                for i, block_ in enumerate((SB, CB)):
                    sp.dma_start(wmod_sb[:, i], wmod_k[:, block_]).then_inc(wmod2_in, 16)
                sp.wait_ge(gates_mm, 1)
                sp.dma_start(x_ring[:, 2], x_t[2]).then_inc(x_in[2], 16)
            sp.wait_ge(gates_ready, 1)
            sp.dma_start(gate_dram.rearrange("g b d -> b g d"), gates[:]).then_inc(gates_out, 16)
            sp.wait_ge(gates_out, 16)
            for b in range(B):
                sp.dma_start(ga_all[:, b], gate_dram[0, b].partition_broadcast(P)).then_inc(ga_in, 16)

            def store_x1(t):
                sp.wait_ge(x1_done, 4 * t + 4)
                sp.dma_start(x1_t[t], x_ring[:, t % X_RING]).then_inc(x1_out, 16)

            def store_h2(t):
                sp.wait_ge(h2_full_done, 4 * t + 4)
                sp.dma_start(h2_dram[t].rearrange("p (k n) -> p k n", k=K), h2_full[:]).then_inc(h2_out, 16)

            for t in range(1, NT):
                store_x1(t - 1)
                if t + 2 < NT:
                    sp.wait_ge(xn2_done, 4 * t)
                    sp.wait_ge(x1_out, 16 * t)
                    sp.dma_start(x_ring[:, (t + 2) % X_RING], x_t[t + 2]).then_inc(x_in[(t + 2) % X_RING], 16)
                store_h2(t - 1)
            store_x1(NT - 1)
            store_h2(NT - 1)
            sp.wait_ge(x1_out, 16 * NT)
            sp.wait_ge(h2_out, 16 * NT)

            def load_w(cm):
                sp.dma_start(w_stage(*cm), w_dram(*cm)).then_inc(w_in[RANK[cm]], 16)

            def load_h2(t2):
                tile = t2 % NT
                sp.dma_start(h2_raw[:], h2_dram[tile].rearrange("p (k n) -> p k n", k=K)).then_inc(h2_in, 16)

            load_w((0, 0))
            sp.dma_start(h2_raw[:], h2_dram[0].rearrange("p (k n) -> p k n", k=K)).then_inc(h2_in, 16)
            load_w((0, 1))
            load_w((1, 0))
            load_w((0, 2))
            load_w((1, 1))
            sp.wait_ge(w_lo_pool, 1)
            load_w((1, 2))
            sp.wait_ge(w_lo_pool, 2)

            def load_y(src, tile):
                sp.dma_start(y[:], src[tile]).then_inc(y_in, 16)
                sp.dma_start(gb_row[:], gate_dram[1, tile // TB].partition_broadcast(P)).then_inc(y_in, 16)

            def store_y(dst, tile, t2):
                sp.wait_ge(y_done, 4 * t2 + 4)
                sp.dma_start(dst[tile], y[:]).then_inc(y_out, 16)
                sp.wait_ge(y_out, 16 * (t2 + 1))

            load_y(x1_t, 0)
            sp.wait_ge(h2_lo_done, 4)
            load_h2(1)
            with sp.Fori(1, NT - 1) as t:
                sp.wait_ge(h2_lo_done, 4 * t + 4)
                load_h2(t + 1)
                store_y(acc_t, t - 1, t - 1)
                load_y(x1_t, t)
            t = NT - 1
            sp.wait_ge(w_lo_pool, 3)
            load_w((2, 0))
            sp.wait_ge(h2_lo_done, 4 * t + 4)
            sp.dma_start(h2_raw[:], h2_dram[0].rearrange("p (k n) -> p k n", k=K)).then_inc(h2_in, 16)
            for i, cm in enumerate(SPLITS[7:9]):
                sp.wait_ge(w_lo_pool, 4 + i)
                load_w(cm)
            store_y(acc_t, t - 1, t - 1)
            load_y(x1_t, t)
            for i, cm in enumerate(SPLITS[9:11]):
                sp.wait_ge(w_lo_pool, 6 + i)
                load_w(cm)
            t = NT
            sp.wait_ge(h2_lo_done, 4 * t + 4)
            sp.dma_start(h2_raw[:], h2_dram[1].rearrange("p (k n) -> p k n", k=K)).then_inc(h2_in, 16)
            sp.wait_ge(w_lo_pool, 8)
            load_w(SPLITS[11])
            store_y(acc_t, NT - 1, t - 1)
            load_y(acc_t, 0)
            with sp.Fori(NT + 1, NT2 - 1) as t:
                sp.wait_ge(h2_lo_done, 4 * t + 4)
                sp.dma_start(h2_raw[:], h2_dram[t - NT + 1].rearrange("p (k n) -> p k n", k=K)).then_inc(h2_in, 16)
                store_y(out_t, t - NT - 1, t - 1)
                load_y(acc_t, t - NT)
            t = NT2 - 1
            store_y(out_t, NT - 2, t - 1)
            load_y(acc_t, NT - 1)
            store_y(out_t, NT - 1, t)

        @block.gpsimd
        def _(pool):
            nc.gpsimd.memset(ident[:], 0.0).then_inc(ident_zero, 1)
            pool.wait_ge(ident_zero, 1)
            nc.gpsimd.affine_select(out=ident[:], in_=ident[:], compare_op=ALU.not_equal, fill=1.0, base=0,
                                    pattern=[[-1, P]], channel_multiplier=1).then_inc(ident_ready, 1)
            pool.wait_ge(wa_hi, 3)
            nc.gpsimd.tensor_tensor(wo_lo[:], h2_full[:], wo_hi[:].bitcast(F32), ALU.subtract).then_inc(wa_lo, 1)

            def sigma_low(t):
                for g in range(K):
                    pool.wait_ge(sigma_hi_done, 4 * t + g + 1)
                    nc.gpsimd.tensor_tensor(sigma_lo[:, g], sigma[:, g], sigma_hi[:, g].bitcast(F32),
                                            ALU.subtract).then_inc(sigma_lo_done, 1)

            def tile(t, first=False, last=False):
                for s in range(S):
                    u = 4 * t + s
                    pool.wait_ge(banks_r_done, 4 * u + 4)
                    nc.gpsimd.tensor_tensor(banks_r[:, :, 0:2], banks_r[:, :, 0:2], banks_r[:, :, 2:4],
                                            ALU.add).then_inc(half_sum_done, 1)
                    pool.wait_ge(half_sum_done, u + 1)
                    if not (first and s == 0):
                        pool.wait_ge(combT_done, u)
                    nc.gpsimd.tensor_tensor(combined[:], banks_r[:, :, 0], banks_r[:, :, 1],
                                            ALU.add).then_inc(comb_done, 1)
                if not last:
                    sigma_low(t + 1)

            sigma_low(0)
            tile(0, first=True)
            with pool.Fori(1, NT - 1) as t:
                tile(t)
            tile(NT - 1, last=True)

            def split_w(cm):
                hi, lo, raw = w_split_views(*cm)
                pool.wait_ge(w_hi_done, RANK[cm] + 1)
                nc.gpsimd.tensor_tensor(lo[:], raw, hi[:].bitcast(F32), ALU.subtract).then_inc(w_lo_pool, 1)

            def h2_low(t2):
                for k in range(K):
                    pool.wait_ge(h2_hi_done, 4 * t2 + k + 1)
                    nc.gpsimd.tensor_tensor(h2_lo[:, k], h2_raw[:, k], h2_hi[:, k].bitcast(F32),
                                            ALU.subtract).then_inc(h2_lo_done, 1)

            def hs_low(n):
                for j in range(J):
                    pool.wait_ge(hs_hi_done, 4 * n + j + 1)
                    nc.gpsimd.tensor_tensor(hs_lo[:, j], h_abs[:, j], hs_hi[:, j].bitcast(F32),
                                            ALU.subtract).then_inc(hs_lo_done, 1)

            def tile_b(t2, first=False, last=False, after0=(), after1=()):
                if not first:
                    hs_low(2 * t2 - 1)
                for cm in after0:
                    split_w(cm)
                hs_low(2 * t2)
                if not last:
                    h2_low(t2 + 1)
                for cm in after1:
                    split_w(cm)

            h2_low(0)
            tile_b(0, first=True, after0=SPLITS[3:6])
            with pool.Fori(1, NT - 1) as t2:
                tile_b(t2)
            tile_b(NT - 1, after0=(), after1=SPLITS[6:8])
            hs_low(2 * NT - 1)
            for cm in SPLITS[8:11]:
                split_w(cm)
            hs_low(2 * NT)
            h2_low(NT + 1)
            split_w(SPLITS[11])
            with pool.Fori(NT + 1, NT2 - 1) as t2:
                tile_b(t2)
            tile_b(NT2 - 1, last=True)
            hs_low(2 * NT2 - 1)

        @block.scalar
        def _(act):
            act.wait_ge(small_in, 16)
            nc.scalar.activation(silu_c[:], cT_sb[:], ACT.Silu).then_inc(silu_c_ready, 1)

            def normalize(t, which, dst, done):
                for s in range(S):
                    nc.scalar.activation(dst[:, s], x_ring[:, t % X_RING, s], ACT.Identity,
                                         bias=ln_shift[:, which, s:s + 1],
                                         scale=ln_rstd[:, which, s:s + 1]).then_inc(done, 1)

            def h1_split(t, first=False, between=lambda: None):
                def full(k):
                    act.wait_ge(t1_done, 4 * t + k + 1)
                    if not (first and k < 2):
                        act.wait_ge(h1_lo_done, 4 * t + k - 1)
                    b = t // TB
                    nc.scalar.activation(h1_full[:, k % 2], bank[6 + k % 2][:], ACT.Identity,
                                         bias=mods[:, 0, k, bass.ds(b, 1)] if not first else mods[:, 0, k, 0:1],
                                         scale=mods[:, 1, k, bass.ds(b, 1)] if not first else mods[:, 1, k, 0:1]
                                         ).then_inc(h1_full_done, 1)

                def hi(k):
                    act.wait_ge(h1_full_done, 4 * t + k + 1)
                    nc.scalar.activation(h1_hi[:, k], h1_full[:, k % 2], ACT.Copy).then_inc(h1_hi_done, 1)

                full(0)
                full(1)
                if not first:
                    act.wait_ge(q_done, 4 * t)
                hi(0)
                hi(1)
                between()
                full(2)
                hi(2)
                full(3)
                hi(3)

            def h2_affine(t, first=False):
                b = t // TB
                for k in range(K):
                    act.wait_ge(t2_done, 4 * t + k + 1)
                    if k == 0 and not first:
                        act.wait_ge(h2_out, 16 * t)
                    nc.scalar.activation(h2_full[:, k], bank[6 + k % 2][:], ACT.Identity,
                                         bias=mods[:, 2, k, bass.ds(b, 1)],
                                         scale=mods[:, 3, k, bass.ds(b, 1)]).then_inc(h2_full_done, 1)

            def sigma_exp(t, g, first=False):
                act.wait_ge(q_done, 4 * t + g + 1)
                if not (first and g < 2):
                    act.wait_ge(sigma_done, 4 * t + g - 1)
                nc.scalar.activation(exp_q[:, g % 2], bank[6 + g % 2][:], ACT.Relu, scale=-1.0).then_inc(neg_done, 1)
                act.wait_ge(neg_done, 4 * t + g + 1)
                nc.scalar.activation(exp_q[:, g % 2], exp_q[:, g % 2], ACT.Exp, scale=-1.0).then_inc(exp_done, 1)

            def sigma_high(t, g):
                act.wait_ge(sigma_done, 4 * t + g + 1)
                nc.scalar.activation(sigma_hi[:, g], sigma[:, g], ACT.Copy).then_inc(sigma_hi_done, 1)

            def sigma_all(t, first=False):
                sigma_exp(t, 0, first)
                sigma_exp(t, 1, first)
                sigma_high(t, 0)
                sigma_exp(t, 2)
                sigma_high(t, 1)
                sigma_exp(t, 3)
                sigma_high(t, 2)
                sigma_high(t, 3)

            def combT_high(u, par, warm=True):
                act.wait_ge(combT_done, u + 1)
                if warm:
                    act.wait_ge(wo_done, u - 1)
                nc.scalar.activation(combT_hi[par][:].rearrange("p k n -> p (k n)"), bank[5][:],
                                     ACT.Copy).then_inc(combT_hi_done, 1)

            act.wait_ge(wq_in, 16)
            nc.scalar.activation(wq_hi[:], banks_r[:].rearrange("p a b c -> p a (b c)"),
                                 ACT.Copy).then_inc(wa_hi, 1)
            act.wait_ge(bank_shifted, 1)
            nc.scalar.activation(bank_sb[:], bank_sb[:], ACT.Exp).then_inc(bank_exp, 1)
            act.wait_ge(var_done, 1)
            nc.scalar.activation(ln_sd[:, 0], ln_var[:, 0], ACT.Sqrt).then_inc(sd_done, 1)
            act.wait_ge(shift_done, 1)
            normalize(0, 0, xn1, xn1_done)
            act.wait_ge(mods_ready, 1)
            h1_split(0, first=True)
            act.wait_ge(mem_bd_ready, 1)
            nc.scalar.activation(mem_hi[:], xn2[:], ACT.Copy).then_inc(wa_hi, 1)
            act.wait_ge(wo_in, 16)
            nc.scalar.activation(wo_hi[:], h2_full[:], ACT.Copy).then_inc(wa_hi, 1)
            sigma_all(0, first=True)

            def tile(t, first=False, last=False):
                for s in range(S):
                    u = 4 * t + s
                    if s == 2:
                        act.wait_ge(var_done, t + 2)
                        a, b = (0, 1) if first else (1, 2) if last else (0, 2)
                        nc.scalar.activation(ln_sd[:, a:b], ln_var[:, a:b], ACT.Sqrt).then_inc(sd_done, 1)
                        act.wait_ge(shift_done, t + 2)
                        if not last:
                            normalize(t + 1, 0, xn1, xn1_done)
                    def transposed():
                        combT_high(u - 1, (s - 1) % 2, warm=not (first and s <= 2))

                    if not (first and s == 0) and (last or s < 3):
                        transposed()
                    if s == 2 and not first:
                        if last:
                            act.wait_ge(shift_done, t + 2)
                        normalize(t - 1, 1, xn2, xn2_done)
                    if s == 3:
                        if not last:
                            h1_split(t + 1, between=transposed)
                        if not first:
                            h2_affine(t - 1)
                if not last:
                    sigma_all(t + 1)

            tile(0, first=True)
            act.wait_ge(wa_lo, 1)
            act.wait_ge(mods_ready, 2)
            with act.Fori(1, NT - 1) as t:
                tile(t)
            tile(NT - 1, last=True)
            combT_high(4 * NT - 1, 1)
            act.wait_ge(var_done, NT + 2)
            nc.scalar.activation(ln_sd[:, 1:2], ln_var[:, 1:2], ACT.Sqrt).then_inc(sd_done, 1)
            act.wait_ge(shift_done, NT + 2)
            normalize(NT - 1, 1, xn2, xn2_done)
            h2_affine(NT - 1)

            def split_w(cm):
                hi, _, raw = w_split_views(*cm)
                act.wait_ge(w_in[RANK[cm]], 16)
                nc.scalar.activation(hi[:], raw, ACT.Copy).then_inc(w_hi_done, 1)

            def h2_high(t2):
                act.wait_ge(h2_in, 16 * (t2 + 1))
                for k in range(K):
                    nc.scalar.activation(h2_hi[:, k], h2_raw[:, k], ACT.Copy).then_inc(h2_hi_done, 1)

            def hs_high(n, first=False):
                if not first:
                    act.wait_ge(down_done, 4 * n)
                for j in range(J):
                    act.wait_ge(kept_done, 4 * n + j + 1)
                    nc.scalar.activation(hs_hi[:, j], h_abs[:, j], ACT.Copy).then_inc(hs_hi_done, 1)

            def silu(n, j, first=False):
                act.wait_ge(gate_done, 4 * n + j + 1)
                if not (first and j < 2):
                    act.wait_ge(h_done, 4 * n + j - 1)
                nc.scalar.activation(silu_g[:, j % 2], bank[2 * (j % 2)][:], ACT.Silu).then_inc(silu_done, 1)

            def absolute(n, j, first=False):
                act.wait_ge(h_done, 4 * n + j + 1)
                if not first:
                    act.wait_ge(hs_lo_done, 4 * n - 4 + j + 1)
                nc.scalar.activation(h_abs[:, j], h_act[:, n_par(n), j], ACT.Abs).then_inc(abs_done, 1)

            par = [0]

            def n_par(n):
                return par[0]

            def item(n, cc, first=False):
                par[0] = cc
                if not first:
                    hs_high(n - 1, first=False)
                silu(n, 0, first)
                silu(n, 1, first)
                absolute(n, 0, first)
                silu(n, 2)
                absolute(n, 1, first)
                silu(n, 3)
                absolute(n, 2, first)
                absolute(n, 3, first)

            def tile_b(t2, last=False):
                item(2 * t2, 0)
                item(2 * t2 + 1, 1)
                if not last:
                    act.wait_ge(up_done, 8 * t2 + 8)
                    h2_high(t2 + 1)

            split_w((0, 0))
            h2_high(0)
            split_w((0, 1))
            split_w((0, 2))
            split_w((1, 0))
            par[0] = 0
            item(0, 0, first=True)
            split_w((1, 1))
            split_w((1, 2))
            par[0] = 1
            act.wait_ge(kept_done, 4)
            for j in range(J):
                nc.scalar.activation(hs_hi[:, j], h_abs[:, j], ACT.Copy).then_inc(hs_hi_done, 1)
            silu(1, 0)
            silu(1, 1)
            absolute(1, 0)
            silu(1, 2)
            absolute(1, 1)
            silu(1, 3)
            absolute(1, 2)
            absolute(1, 3)
            act.wait_ge(up_done, 8)
            h2_high(1)
            with act.Fori(1, NT - 1) as t2:
                tile_b(t2)
            t2 = NT - 1
            item(2 * t2, 0)
            item(2 * t2 + 1, 1)
            act.wait_ge(up_done, 8 * t2 + 8)
            h2_high(t2 + 1)
            split_w(SPLITS[6])
            split_w(SPLITS[7])
            t2 = NT
            item(2 * t2, 0)
            act.wait_ge(down_done, 4 * (2 * NT - 1))
            split_w(SPLITS[8])
            split_w(SPLITS[9])
            split_w(SPLITS[10])
            item(2 * t2 + 1, 1)
            act.wait_ge(up_done, 8 * t2 + 8)
            h2_high(t2 + 1)
            act.wait_ge(down_done, 4 * (2 * NT))
            split_w(SPLITS[11])
            with act.Fori(NT + 1, NT2 - 1) as t2:
                tile_b(t2)
            tile_b(NT2 - 1, last=True)
            hs_high(2 * NT2 - 1)

        @block.vector
        def _(dve):
            chain = [0]

            def link(ins):
                chain[0] += 1
                ins.then_inc(setup_dve, 1)
                dve.wait_ge(setup_dve, chain[0])

            def ln_stats(t, which, s, done):
                nc.vector.bn_stats(ln_raw[:, which, s], x_ring[:, t % X_RING, s]).then_inc(done, 1)

            def ln_aggregate(t, which, ag):
                for s in range(S):
                    nc.vector.bn_aggr(ln_mv[:, which, s], ln_raw[:, which, s]).then_inc(ag, 1)
                dve.wait_ge(ag, 4 * t + 4)

            def ln_variance(a, b):
                return nc.vector.tensor_scalar(ln_var[:, a:b], ln_mv[:, a:b, :, 1], LN_EPS, None, ALU.add)

            def ln_scalars(step, a, b):
                dve.wait_ge(sd_done, step)
                nc.vector.reciprocal(ln_rstd[:, a:b], ln_sd[:, a:b]).then_inc(rstd_done, 1)
                dve.wait_ge(rstd_done, step)
                for w in range(a, b):
                    ins = nc.vector.scalar_tensor_tensor(out=ln_shift[:, w], in0=ln_mv[:, w, :, 0], scalar=-1.0,
                                                         in1=ln_rstd[:, w], op0=ALU.mult, op1=ALU.mult)
                ins.then_inc(shift_done, 1)

            def h1_low(t, blocks=range(K)):
                for k in blocks:
                    dve.wait_ge(h1_hi_done, 4 * t + k + 1)
                    nc.vector.tensor_tensor(h1_lo[:, k], h1_full[:, k % 2], h1_hi[:, k].bitcast(F32),
                                            ALU.subtract).then_inc(h1_lo_done, 1)

            def sigma_of(t):
                for g in range(K):
                    dve.wait_ge(exp_done, 4 * t + g + 1)
                    nc.vector.scalar_tensor_tensor(out=sigma[:, g], in0=bank[6 + g % 2][:], scalar=0.0,
                                                   in1=exp_q[:, g % 2], op0=ALU.max,
                                                   op1=ALU.add).then_inc(sigma_done, 1)

            nc.vector.memset(ones[:], 1.0).then_inc(consts_ready, 1)
            nc.vector.memset(xn2[:], 0.0)
            link(nc.vector.memset(norm_bd[:], 0.0))
            dve.wait_ge(x_in[0], 16)
            for s in range(S):
                ln_stats(0, 0, s, bn1_done)
            dve.wait_ge(bn1_done, 4)
            ln_aggregate(0, 0, ag1_done)
            ln_variance(0, 1).then_inc(var_done, 1)
            dve.wait_ge(wa_hi, 1)
            nc.vector.tensor_tensor(wq_lo[:], banks_r[:].rearrange("p a b c -> p a (b c)"),
                                    wq_hi[:].bitcast(F32), ALU.subtract)
            dve.wait_ge(norm_in, 48)
            link(nc.vector.tensor_reduce(bank_red[:], bank_sb[:], AX_X, ALU.max))
            nc.vector.tensor_tensor(bank_sb[:], bank_sb[:], bank_red[:].unsqueeze(2).broadcast_to([P, K * HG, NB]),
                                    ALU.subtract).then_inc(bank_shifted, 1)
            ln_scalars(1, 0, 1)
            mem_bd = xn2[:].rearrange("p k (n h e) -> p k n h e", n=NB, h=HG)
            for hh in range(HG):
                rows = slice(DH * hh, DH * hh + DH)
                for k in range(K):
                    nc.vector.tensor_copy(mem_bd[rows, k, :, hh, :], mem_raw[rows, k])
                ins = nc.vector.tensor_copy(norm_bd[rows, :, :, hh], norm_raw[rows])
            ins.then_inc(mem_bd_ready, 1)
            dve.wait_ge(mods_mm, 1)
            mm = bank[7][:, 0:4 * K * B].rearrange("p (i k b) -> p i k b", i=4, k=K)
            nc.vector.tensor_copy(mods[:, 0], mm[:, 0])
            nc.vector.tensor_scalar(mods[:, 1], mm[:, 1], 1.0, None, ALU.add).then_inc(mods_ready, 1)
            h1_low(0)
            dve.wait_ge(bank_exp, 1)
            link(nc.vector.tensor_reduce(bank_red[:], bank_sb[:], AX_X, ALU.add))
            link(nc.vector.reciprocal(bank_red[:], bank_red[:]))
            link(nc.vector.tensor_tensor(bank_sb[:], bank_sb[:],
                                         bank_red[:].unsqueeze(2).broadcast_to([P, K * HG, NB]), ALU.mult))
            dve.wait_ge(active_mm, 1)
            link(nc.vector.tensor_reduce(active_sum[:],
                                         bank[5][:, 0:K * NB].rearrange("p (k n) -> p n k", k=K), AX_X, ALU.add))
            link(nc.vector.tensor_scalar(active_sum[:], active_sum[:], NORM_EPS, None, ALU.is_ge))
            for k in range(K):
                ins = nc.vector.tensor_tensor(bank_gate[:, k],
                                              bank_sb[:, HG * k:HG * k + HG].rearrange("p h n -> p n h"),
                                              active_sum[:].unsqueeze(2).broadcast_to([P, NB, HG]), ALU.mult)
            link(ins)
            dve.wait_ge(wa_hi, 2)
            nc.vector.tensor_tensor(mem_lo[:], xn2[:], mem_hi[:].bitcast(F32), ALU.subtract).then_inc(gate_ready, 1)
            sigma_of(0)
            dve.wait_ge(mods_mm, 2)
            nc.vector.tensor_copy(mods[:, 2], mm[:, 2])
            nc.vector.tensor_scalar(mods[:, 3], mm[:, 3], 1.0, None, ALU.add).then_inc(mods_ready, 1)
            dve.wait_ge(gates_mm, 2)
            gate_abs = banks_r[0:B, 0:2].rearrange("b i n c -> b i (n c)")
            for i in range(2):
                nc.vector.tensor_copy(gates[:, i], bank[3 + i][0:B, :]).then_inc(setup_dve, 1)
            chain[0] += 2
            dve.wait_ge(setup_dve, chain[0])
            link(nc.vector.scalar_tensor_tensor(out=gate_abs, in0=gates[:], scalar=-1.0, in1=gates[:],
                                                op0=ALU.mult, op1=ALU.max))
            link(nc.vector.tensor_scalar(gate_abs, gate_abs, 0.25, None, ALU.max))
            link(nc.vector.tensor_scalar(gates[:], gates[:], 0.0, 2.0, ALU.is_ge, ALU.mult))
            nc.vector.scalar_tensor_tensor(out=gates[:], in0=gates[:], scalar=-1.0, in1=gate_abs,
                                           op0=ALU.add, op1=ALU.mult).then_inc(gates_ready, 1)

            def attn_rest(tp, sp_, u):
                dve.wait_ge(wo_done, u + 1)
                b = tp // TB
                nc.vector.tensor_tensor(attn_scaled[:], bank[4][:], ga_all[:, b], ALU.mult
                                        ).then_inc(attn_scaled_done, 1)
                dve.wait_ge(attn_scaled_done, u + 1)
                xs = x_ring[:, tp % X_RING, sp_]
                nc.vector.tensor_tensor(xs, xs, attn_scaled[:], ALU.add).then_inc(x1_done, 1)
                dve.wait_ge(x1_done, u + 1)
                ln_stats(tp, 1, sp_, bn2_done)

            def combT_low(u, par):
                dve.wait_ge(combT_hi_done, u + 1)
                nc.vector.tensor_tensor(combT_lo[par][:].rearrange("p k n -> p (k n)"), bank[5][:],
                                        combT_hi[par][:].rearrange("p k n -> p (k n)").bitcast(F32),
                                        ALU.subtract).then_inc(combT_lo_done, 1)

            def tile(t, x_wait, first=False, last=False):
                for s in range(S):
                    u = 4 * t + s
                    inv = inv_norm[:, s % 2]
                    dve.wait_ge(norm_done, u + 1)
                    nc.vector.tensor_scalar(inv, bank[6][:, 0:K * NB * HG], NORM_EPS, None,
                                            ALU.max).then_inc(clip_done, 1)
                    dve.wait_ge(clip_done, u + 1)
                    nc.vector.reciprocal(inv, inv).then_inc(recip_done, 1)
                    dve.wait_ge(recip_done, u + 1)
                    nc.vector.tensor_tensor(inv, inv,
                                            bank_gate[:].rearrange("p k n h -> p (k n h)"),
                                            ALU.mult).then_inc(r_done, 1)
                    dve.wait_ge(r_done, u + 1)
                    if not (first and s == 0):
                        dve.wait_ge(comb_done, u)
                    for g in range(K):
                        dve.wait_ge(banks_done, 4 * u + g + 1)
                        r = inv[:, g * NB * HG:(g + 1) * NB * HG]
                        nc.vector.tensor_tensor(
                            banks_r[:, g].rearrange("p n (h e) -> p (n h) e", h=HG),
                            bank[g][:].rearrange("p (a e) -> p a e", e=DH),
                            r.unsqueeze(2).broadcast_to([P, NB * HG, DH]), ALU.mult).then_inc(banks_r_done, 1)
                    if s < 2 and not last:
                        if s == 0:
                            x_wait()
                        for i in range(2):
                            ln_stats(t + 1, 0, 2 * s + i, bn1_done)
                    if s == 2:
                        a, b = (0, 1) if first else (1, 2) if last else (0, 2)
                        ln_scalars(t + 2, a, b)
                    if s == 1 and not last:
                        dve.wait_ge(bn1_done, 4 * t + 8)
                    if s == 3 and not last:
                        h1_low(t + 1, (0, 1))
                    if not (first and s == 0):
                        combT_low(u - 1, (s - 1) % 2)
                    if s == 3 and not last:
                        h1_low(t + 1, (2, 3))
                    if not (first and s < 2):
                        if first and s == 2:
                            dve.wait_ge(ga_in, 16 * B)
                        attn_rest(t - 1 if s < 2 else t, (s - 2) % S, u - 2)
                    if s == 1:
                        if not last:
                            ln_aggregate(t + 1, 0, ag1_done)
                            if not first:
                                dve.wait_ge(bn2_done, 4 * t)
                            ins = ln_variance(0, 1)
                        if not first:
                            if last:
                                dve.wait_ge(bn2_done, 4 * t)
                            ln_aggregate(t - 1, 1, ag2_done)
                            ins = ln_variance(1, 2)
                        ins.then_inc(var_done, 1)
                if not last:
                    sigma_of(t + 1)

            def wait_x(t):
                dve.wait_ge(x_in[t % X_RING], 16 * (t // X_RING + 1))

            tile(0, lambda: wait_x(1), first=True)
            with dve.Fori(0, (NT - 2) // X_RING) as r:
                for i in range(X_RING):
                    nxt = 2 + i
                    fills = r + (1 + nxt // X_RING)
                    tile(r * X_RING + (1 + i), lambda: dve.wait_ge(x_in[nxt % X_RING], fills * 16))
            tile(NT - 1, None, last=True)
            combT_low(4 * NT - 1, 1)
            attn_rest(NT - 1, 2, 4 * NT - 2)
            attn_rest(NT - 1, 3, 4 * NT - 1)
            dve.wait_ge(bn2_done, 4 * NT)
            ln_aggregate(NT - 1, 1, ag2_done)
            ln_variance(1, 2).then_inc(var_done, 1)
            ln_scalars(NT + 2, 1, 2)

            for cm in SPLITS[0:3]:
                hi, lo, raw = w_split_views(*cm)
                dve.wait_ge(w_hi_done, RANK[cm] + 1)
                nc.vector.tensor_tensor(lo[:], raw, hi[:].bitcast(F32), ALU.subtract).then_inc(w_lo_dve, 1)

            def hidden_act(n, cc, j):
                dve.wait_ge(silu_done, 4 * n + j + 1)
                dve.wait_ge(up_done, 4 * n + j + 1)
                nc.vector.tensor_tensor(h_act[:, cc, j], bank[2 * (j % 2) + 1][:], silu_g[:, j % 2],
                                        ALU.mult).then_inc(h_done, 1)

            MASK_STEPS = 10

            def sparsify(n, cc):
                def step(ins):
                    ins.then_inc(mask_step, 1)

                def done(i):
                    dve.wait_ge(mask_step, MASK_STEPS * n + i)

                even, odd = h_abs[:, 0:J:2], h_abs[:, 1:J:2]
                dve.wait_ge(abs_done, 4 * n + 4)
                step(nc.vector.tensor_tensor(pair_hi[:], even, odd, ALU.max))
                step(nc.vector.tensor_tensor(pair_lo[:], even, odd, ALU.min))
                step(nc.vector.tensor_tensor(first_wins[:], even, odd, ALU.is_ge))
                done(2)
                step(nc.vector.tensor_tensor(both_of[:, 0], pair_lo[:, 0], pair_hi[:, 1], ALU.is_ge))
                step(nc.vector.tensor_tensor(both_of[:, 1], pair_lo[:, 1], pair_hi[:, 0], ALU.is_gt))
                done(5)
                step(nc.vector.tensor_tensor(one_each[:, 0], both_of[:, 0], both_of[:, 1], ALU.is_equal))
                done(6)
                step(nc.vector.tensor_tensor(first_wins[:], first_wins[:],
                                             one_each[:].broadcast_to([P, 2, T]), ALU.mult))
                done(7)
                step(nc.vector.tensor_tensor(keep[:, 0:J:2], both_of[:], first_wins[:], ALU.add))
                step(nc.vector.tensor_tensor(keep[:, 1], both_of[:, 1], first_wins[:, 0], ALU.is_equal))
                step(nc.vector.tensor_tensor(keep[:, 3], both_of[:, 0], first_wins[:, 1], ALU.is_equal))
                done(10)
                for j in range(J):
                    nc.vector.tensor_tensor(h_abs[:, j], keep[:, j], h_act[:, cc, j],
                                            ALU.mult).then_inc(kept_done, 1)

            def add_ffn(t2):
                dve.wait_ge(y_in, 32 * (t2 + 1))
                for s in range(S):
                    dve.wait_ge(down_done, 4 * (2 * t2 + 1) + s + 1)
                    nc.vector.tensor_tensor(ffn_scaled[:, s % 2], bank[4 + s][:], gb_row[:],
                                            ALU.mult).then_inc(y_scaled, 1)
                    dve.wait_ge(y_scaled, 4 * t2 + s + 1)
                    nc.vector.tensor_tensor(y[:, s], y[:, s], ffn_scaled[:, s % 2], ALU.add).then_inc(y_done, 1)

            def tile_b(t2, first=False):
                for cc in range(SLOTS):
                    n = 2 * t2 + cc
                    for j in range(J):
                        hidden_act(n, cc, j)
                        if cc == 1 and j == 1 and not first:
                            add_ffn(t2 - 1)
                    sparsify(n, cc)

            tile_b(0, first=True)
            with dve.Fori(1, NT2) as t2:
                tile_b(t2)
            add_ffn(NT2 - 1)

        @block.tensor
        def _(pe):
            def mm3(out_, stat, mov, start, stop):
                nc.tensor.matmul(out_, stat[0], mov[0], start=start, stop=False)
                nc.tensor.matmul(out_, stat[0], mov[1], start=False, stop=False)
                return nc.tensor.matmul(out_, stat[1], mov[0], start=False, stop=stop)

            def mod_scalars(i, at_block):
                for f in range(K):
                    for k in range(K):
                        at = (i * K + f) * B
                        ins = nc.tensor.matmul(bank[7][:, at:at + B],
                                               wmod_sb[:, at_block, k, f * P:(f + 1) * P], silu_c[:, k],
                                               start=(k == 0), stop=(k == K - 1))
                return ins

            pe.wait_ge(silu_c_ready, 1)
            pe.wait_ge(wmod1_in, 32)
            mod_scalars(0, 0)
            mod_scalars(1, 1).then_inc(mods_mm, 1)

            def ln_transpose(src, t, k, done):
                for s in range(S):
                    ins = nc.tensor.transpose(bank[6 + k % 2][:, s * P:(s + 1) * P], src[:, s, k * P:(k + 1) * P],
                                              ident[:])
                ins.then_inc(done, 1)

            def t1(t, k, first=False):
                if k == 0:
                    pe.wait_ge(xn1_done, 4 * t + 4)
                if k >= 2:
                    pe.wait_ge(h1_full_done, 4 * t + k - 1)
                ln_transpose(xn1, t, k, t1_done)

            def t2(t, k):
                if k == 0:
                    pe.wait_ge(xn2_done, 4 * t + 4)
                if k >= 2:
                    pe.wait_ge(h2_full_done, 4 * t + k - 1)
                ln_transpose(xn2, t, k, t2_done)

            def q_block(t, g):
                if g >= 2:
                    pe.wait_ge(sigma_done, 4 * t + g - 1)
                for k in range(K):
                    if g == 0:
                        pe.wait_ge(h1_lo_done, 4 * t + k + 1)
                    ins = mm3(bank[6 + g % 2][:], (wq_hi[:, k, g * P:(g + 1) * P], wq_lo[:, k, g * P:(g + 1) * P]),
                              (h1_hi[:, k], h1_lo[:, k]), k == 0, k == K - 1)
                ins.then_inc(q_done, 1)

            def norms(t, s, first=False):
                u = 4 * t + s
                if s == 0:
                    pe.wait_ge(sigma_done, 4 * t + 4)
                else:
                    pe.wait_ge(clip_done, u)
                for g in range(K):
                    cols = slice(g * NB * HG, (g + 1) * NB * HG)
                    ins = nc.tensor.matmul(bank[6][:, cols], sigma[:, g, s * P:(s + 1) * P],
                                           norm_bd[:, g].rearrange("p n h -> p (n h)"), start=True, stop=True)
                ins.then_inc(norm_done, 1)

            def banks_of(t, s, first=False):
                u = 4 * t + s
                for g in range(K):
                    if s == 0:
                        pe.wait_ge(sigma_lo_done, 4 * t + g + 1)
                    if not (first and s == 0):
                        pe.wait_ge(banks_r_done, 4 * u - 3 + g)
                    mm3(bank[g][:], (sigma_hi[:, g, s * P:(s + 1) * P], sigma_lo[:, g, s * P:(s + 1) * P]),
                        (mem_hi[:, g], mem_lo[:, g]), True, True).then_inc(banks_done, 1)

            def comb_transpose(u, first=False):
                pe.wait_ge(comb_done, u + 1)
                if not first:
                    pe.wait_ge(combT_lo_done, u)
                for g in range(K):
                    ins = nc.tensor.transpose(bank[5][:, g * P:(g + 1) * P], combined[:, g], ident[:])
                ins.then_inc(combT_done, 1)

            def wo_product(u, par, first=False):
                pe.wait_ge(combT_lo_done, u + 1)
                if not first:
                    pe.wait_ge(attn_scaled_done, u)
                for g in range(K):
                    ins = mm3(bank[4][:], (combT_hi[par][:, g], combT_lo[par][:, g]),
                              (wo_hi[:, g], wo_lo[:, g]), g == 0, g == K - 1)
                ins.then_inc(wo_done, 1)

            pe.wait_ge(ident_ready, 1)
            for k in range(K):
                if k == 1:
                    pe.wait_ge(mods_ready, 1)
                t1(0, k)
            pe.wait_ge(consts_ready, 1)
            pe.wait_ge(norm_in, 48)
            nc.tensor.matmul(bank[5][:, 0:K * NB], ones[:], norm_raw[:].rearrange("p k n -> p (k n)"),
                             start=True, stop=True).then_inc(active_mm, 1)
            pe.wait_ge(wa_hi, 1)
            for g in range(K):
                if g < 2:
                    pe.wait_ge(h1_full_done, 3 + g)
                q_block(0, g)
            pe.wait_ge(sigma_done, 4)
            pe.wait_ge(wmod2_in, 32)
            mod_scalars(2, 0)
            mod_scalars(3, 1).then_inc(mods_mm, 1)
            pe.wait_ge(wmod_gates_in, 32)
            for i, gate_w in enumerate((x_ring[:, 2], wmod_sb[:, 2])):
                for k in range(K):
                    ins = nc.tensor.matmul(bank[3 + i][0:B, :], silu_c[:, k], gate_w[:, k],
                                           start=(k == 0), stop=(k == K - 1))
                ins.then_inc(gates_mm, 1)
            pe.wait_ge(gates_ready, 1)
            pe.wait_ge(mods_ready, 2)
            pe.wait_ge(gate_ready, 1)
            pe.wait_ge(wa_lo, 1)

            def tile(t, first=False, last=False):
                for s in range(S):
                    u = 4 * t + s
                    norms(t, s, first)
                    banks_of(t, s, first)
                    t1_here = s == 3 and not last
                    if s == 3:
                        pe.wait_ge(clip_done, u + 1)
                    if t1_here:
                        t1(t + 1, 0)
                        t1(t + 1, 1)
                    if not (first and s < 2):
                        wo_product(u - 2, s % 2, first=(first and s == 2))
                    if not (first and s == 0):
                        comb_transpose(u - 1, first=(first and s == 1))
                    if t1_here:
                        t1(t + 1, 2)
                        t1(t + 1, 3)
                    if s == 3 and not first:
                        for k in range(K):
                            if not last and k < 2:
                                pe.wait_ge(h1_full_done, 4 * t + 4 + k + 3)
                            t2(t - 1, k)
                if not last:
                    for g in range(K):
                        if g < 2:
                            if first:
                                pe.wait_ge(h1_full_done, 4 * t + 4 + g + 3)
                            else:
                                pe.wait_ge(h2_full_done, 4 * t - 4 + g + 3)
                        q_block(t + 1, g)

            tile(0, first=True)
            with pe.Fori(1, NT - 1) as t:
                tile(t)
            tile(NT - 1, last=True)
            wo_product(4 * NT - 2, 0)
            comb_transpose(4 * NT - 1)
            wo_product(4 * NT - 1, 1)
            for k in range(K):
                if k < 2:
                    pe.wait_ge(h2_full_done, 4 * (NT - 2) + k + 3)
                t2(NT - 1, k)

            def gate_up(t2, cc, chunk, first=False):
                n = 2 * t2 + cc
                w_lo_wait(pe, (chunk, 0))
                for j in range(J):
                    for m, (hi, lo) in enumerate(((w_gate_hi, w_gate_lo), (w_up_hi, w_up_lo))):
                        if j == 0 and m == 1:
                            w_lo_wait(pe, (chunk, 1))
                        if not (first and j < 2):
                            pe.wait_ge((silu_done, h_done)[m], 4 * n + j - 1)
                        for k in range(K):
                            if cc == 0 and j == 0 and m == 0:
                                pe.wait_ge(h2_lo_done, 4 * t2 + k + 1)
                            ins = mm3(bank[2 * (j % 2) + m][:], (hi[cc][:, k, j], lo[cc][:, k, j]),
                                      (h2_hi[:, k], h2_lo[:, k]), k == 0, k == K - 1)
                        ins.then_inc((gate_done, up_done)[m], 1)

            def down(t2, cc, chunk, first=False):
                n = 2 * t2 + cc
                w_lo_wait(pe, (chunk, 2))
                if cc == 0 and not first:
                    pe.wait_ge(y_scaled, 4 * t2)
                for s in range(S):
                    for j in range(J):
                        if s == 0:
                            pe.wait_ge(hs_lo_done, 4 * n + j + 1)
                        cols = slice(s * P, (s + 1) * P)
                        ins = mm3(bank[4 + s][:], (hs_hi[:, j, cols], hs_lo[:, j, cols]),
                                  (w_down_hi[cc][:, j], w_down_lo[cc][:, j]),
                                  cc == 0 and j == 0, cc == SLOTS - 1 and j == J - 1)
                    ins.then_inc(down_done, 1)

            def tile_b(t2, pass_, prev_pass, first=False):
                gate_up(t2, 0, 2 * pass_, first)
                if not first:
                    down(t2 - 1, 1, 2 * prev_pass + 1)
                gate_up(t2, 1, 2 * pass_ + 1)
                down(t2, 0, 2 * pass_, first)

            tile_b(0, 0, 0, first=True)
            with pe.Fori(1, NT) as t2_:
                tile_b(t2_, 0, 0)
            tile_b(NT, 1, 0)
            with pe.Fori(NT + 1, NT2) as t2_:
                tile_b(t2_, 1, 1)
            down(NT2 - 1, 1, CHUNKS - 1)


_INS = ["x", "wqT", "woT", "bank_w", "mem_hd", "norm_hd", "w_gate", "w_up", "w_down", "cT", "wmod"]


def kernel(**inputs):
    import numpy as _np
    import concourse.bacc as _bacc
    from concourse import mybir as _mybir
    from concourse.bass_utils import run_bass_kernel_spmd as _run

    a = {n: _np.asarray(v) for n, v in inputs.items()}
    x = a["L0_attn_hidden_states"]
    b, s, d = x.shape
    mem, norm = a["L0_attn_memories"], a["L0_attn_memory_norms"]
    nb, h, dh, _ = mem.shape
    laid = {
        "x": x.reshape(b * s, d),
        "wqT": a["L0_attn_Wq"].T,
        "woT": a["L0_attn_Wo"].T,
        "bank_w": a["L0_attn_bank_weights"],
        "mem_hd": mem.transpose(1, 2, 0, 3).reshape(h * dh, nb, dh),
        "norm_hd": norm.transpose(1, 2, 0).reshape(h * dh, nb),
        "w_gate": a["L0_ffn_w_gate"],
        "w_up": a["L0_ffn_w_up"],
        "w_down": a["L0_ffn_w_down"],
        "cT": a["L0_c"].T,
        "wmod": a["L0_wmod"],
    }
    nc = _bacc.Bacc("TRN2", target_bir_lowering=False, num_devices=1)
    arrays, args = {}, []
    for name in _INS:
        v = _np.ascontiguousarray(laid[name])
        arrays[f"in_{name}_dram"] = v
        args.append(nc.dram_tensor(f"in_{name}_dram", v.shape, _mybir.dt.from_np(v.dtype), kind="ExternalInput").ap())
    out = nc.dram_tensor("out_dram", (b * s, d), _mybir.dt.float32, kind="ExternalOutput").ap()
    adaln_kernel(nc, *args, out)
    r = _run(nc, [arrays], core_ids=[0])
    return r.results[0]["out_dram"].reshape(b, s, d)
```

```python
from contextlib import ExitStack

import concourse.bass as bass
from concourse import mybir

F32 = mybir.dt.float32
F32R = mybir.dt.float32r
BF16 = mybir.dt.bfloat16
ALU = mybir.AluOpType
ACT = mybir.ActivationFunctionType
AX_X = mybir.AxisListType.X

P = 128
D = 512
T = 512
S = T // P
SLOTS = 2
K = D // P
B = 4
NB = 4
DH = 32
HG = P // DH
J = 4
CH = 512
LN_EPS = 1e-5
NORM_EPS = 1e-6
X_RING = 3
SA, CA, GA, SB, CB, GB = range(6)


def adaln_kernel(nc, x, wqT, woT, bank_w, mem_hd, norm_hd, w_gate, w_up, w_down, cT, wmod, out):
    tokens = x.shape[0]
    NT = tokens // T
    TB = NT // B
    hidden = w_gate.shape[1]
    CHUNKS = hidden // CH
    PASSES = CHUNKS // SLOTS
    NT2 = NT * PASSES

    x1_dram = nc.dram_tensor("x1_scratch", (tokens, D), F32, kind="Internal").ap()
    acc_dram = nc.dram_tensor("acc_scratch", (tokens, D), F32, kind="Internal").ap()
    h2_dram = nc.dram_tensor("h2T_scratch", (NT, P, K * T), F32, kind="Internal").ap()
    gate_dram = nc.dram_tensor("gates_scratch", (2, B, D), F32, kind="Internal").ap()

    def tiled(dram):
        return dram.rearrange("(t p s) d -> t p s d", p=P, s=S)

    x_t, x1_t, acc_t, out_t = tiled(x), tiled(x1_dram), tiled(acc_dram), tiled(out)

    with ExitStack() as ctx:
        def sem(name):
            return ctx.enter_context(nc.semaphore(name))

        bank = [ctx.enter_context(nc.psum_tensor(f"bank{i}", [P, 512], F32)) for i in range(8)]

        w_raw = ctx.enter_context(nc.sbuf_tensor("w_raw", [P, K * CH], F32))

        with ExitStack() as phase_a:
            def sba(name, shape, dt=F32):
                return phase_a.enter_context(nc.sbuf_tensor(name, shape, dt))

            wq_hi = sba("wq_hi", [P, K, D], F32R)
            wq_lo = sba("wq_lo", [P, K, D], F32R)
            h1_hi = sba("h1_hi", [P, K, T], F32R)
            h1_lo = sba("h1_lo", [P, K, T], F32R)
            xn1 = sba("xn1", [P, S, D])
            h1_full = sba("h1_full", [P, 2, T])
            exp_q = sba("exp_q", [P, 2, T])
            x_ring = sba("x_ring", [P, X_RING, S, D])
            sigma = sba("sigma", [P, K, T])
            sigma_hi = sba("sigma_hi", [P, K, T], F32R)
            sigma_lo = sba("sigma_lo", [P, K, T], F32R)
            mem_hi = sba("mem_hi", [P, K, NB * P], F32R)
            mem_lo = sba("mem_lo", [P, K, NB * P], F32R)
            banks_r0 = sba("banks_r0", [P, K, NB, P])
            with ExitStack() as setup_only:
                wmod_sb = setup_only.enter_context(nc.sbuf_tensor("wmod_sb", [P, 2, K, D], F32))
            banks_r = [banks_r0, sba("banks_r1", [P, K, NB, P])]
            combT_hi = [sba(f"combT_hi{i}", [P, K, P], F32R) for i in range(2)]
            combT_lo = [sba(f"combT_lo{i}", [P, K, P], F32R) for i in range(2)]
            combined = sba("combined", [P, K, P])
            attn_scaled = sba("attn_scaled", [P, D])
            xn2 = sba("xn2", [P, S, D])
            h2_full = sba("h2_full", [P, K, T])
            wo_hi = sba("wo_hi", [P, K, D], F32R)
            wo_lo = sba("wo_lo", [P, K, D], F32R)
            ga_all = sba("ga_all", [P, B, D])
            ident = sba("ident", [P, P])
            ones = sba("ones", [P, P])
            mem_raw = sba("mem_raw", [P, K, NB, DH])
            norm_raw = sba("norm_raw", [P, K, NB])
            norm_bd = sba("norm_bd", [P, K, NB, HG])
            bank_sb = sba("bank_sb", [P, K * HG, NB])
            bank_red = sba("bank_red", [P, K * HG])
            active_sum = sba("active_sum", [P, NB])
            bank_gate = sba("bank_gate", [P, K, NB, HG])
            inv_norm = sba("inv_norm", [P, 2, K * NB * HG])
            cT_sb = sba("cT_sb", [P, K, B])
            silu_c = sba("silu_c", [P, K, B])
            mods = sba("mods", [P, 4, K, B])
            gates = sba("gates", [B, 2, D])
            ln_raw = sba("ln_raw", [P, 2, S, 6])
            ln_mv = sba("ln_mv", [P, 2, S, 2])
            ln_var = sba("ln_var", [P, 2, S])
            ln_sd = sba("ln_sd", [P, 2, S])
            ln_rstd = sba("ln_rstd", [P, 2, S])
            ln_shift = sba("ln_shift", [P, 2, S])

        def sbb(name, shape, dt=F32):
            return ctx.enter_context(nc.sbuf_tensor(name, shape, dt))

        def in_halves(name, shape):
            return [sbb(f"{name}_hi", shape, F32R), sbb(f"{name}_lo", shape, F32R)]

        gate_w, up_w, down_w = [None] * SLOTS, [None] * SLOTS, [None] * SLOTS
        gate_w[0] = in_halves("gate_w0", [P, K, J, P])
        up_w[0] = in_halves("up_w0", [P, K, J, P])
        h2_raw = sbb("h2_raw", [P, K, T])
        h2_hi = sbb("h2_hi", [P, K, T], F32R)
        h2_lo = sbb("h2_lo", [P, K, T], F32R)
        over_x1 = sbb("over_x1", [P, 2, S, D])
        silu_g = sbb("silu_g", [P, 2, T])
        h_act = sbb("h_act", [P, SLOTS, J, T])
        h_abs = sbb("h_abs", [P, J, T])
        pair_hi = sbb("pair_hi", [P, 2, T])
        pair_lo = sbb("pair_lo", [P, 2, T])
        first_wins = sbb("first_wins", [P, 2, T], BF16)
        both_of = sbb("both_of", [P, 2, T], BF16)
        one_each = sbb("one_each", [P, 1, T], BF16)
        keep = sbb("keep", [P, J, T], BF16)
        hs_hi = sbb("hs_hi", [P, J, T], F32R)
        hs_lo = sbb("hs_lo", [P, J, T], F32R)
        y = over_x1[:, 0]
        over_x1_rest = over_x1[:, 1]
        gb_row = over_x1_rest[:, 0]
        ffn_scaled = over_x1_rest[:, 1:3]
        down_w[0] = in_halves("down_w0", [P, J, D])
        gate_w[1] = in_halves("gate_w1", [P, K, J, P])
        up_w[1] = in_halves("up_w1", [P, K, J, P])
        down_w[1] = in_halves("down_w1", [P, J, D])

        small_in, norm_in, wmod1_in, wmod2_in, wmod_gates_in, wq_in, wo_in = map(sem, (
            "small_in", "norm_in", "wmod1_in", "wmod2_in", "wmod_gates_in", "wq_in", "wo_in"))
        x_in = [sem(f"x_in{i}") for i in range(X_RING)]
        gates_out, ga_in, x1_out, h2_out = map(sem, ("gates_out", "ga_in", "x1_out", "h2_out"))
        ident_zero, ident_ready, consts_ready, setup_dve = map(sem, (
            "ident_zero", "ident_ready", "consts_ready", "setup_dve"))
        silu_c_ready, mods_mm, gates_mm, active_mm, mods_ready, gates_ready = map(sem, (
            "silu_c_ready", "mods_mm", "gates_mm", "active_mm", "mods_ready", "gates_ready"))
        bank_shifted, bank_exp, mem_bd_ready, wa_hi, wa_lo, gate_ready = map(sem, (
            "bank_shifted", "bank_exp", "mem_bd_ready", "wa_hi", "wa_lo", "gate_ready"))
        bn1_done, ag1_done, bn2_done, ag2_done = map(sem, ("bn1_done", "ag1_done", "bn2_done", "ag2_done"))
        var_done, sd_done, rstd_done, shift_done = (
            [sem(f"{name}{i + 1}") for i in range(2)] for name in ("var_done", "sd_done", "rstd_done", "shift_done"))
        xn1_done, t1_done, h1_full_done, h1_hi_done, h1_lo_done = map(sem, (
            "xn1_done", "t1_done", "h1_full_done", "h1_hi_done", "h1_lo_done"))
        q_done, exp_done, neg_done, sigma_done, sigma_hi_done, sigma_lo_done = map(sem, (
            "q_done", "exp_done", "neg_done", "sigma_done", "sigma_hi_done", "sigma_lo_done"))
        norm_done, clip_done, recip_done, r_done = map(sem, ("norm_done", "clip_done", "recip_done", "r_done"))
        banks_done, banks_r_done, half_sum_done, comb_done = map(sem, (
            "banks_done", "banks_r_done", "half_sum_done", "comb_done"))
        combT_done, combT_hi_done, combT_lo_done = map(sem, ("combT_done", "combT_hi_done", "combT_lo_done"))
        wo_done, attn_scaled_done, x1_done = map(sem, ("wo_done", "attn_scaled_done", "x1_done"))
        xn2_done, t2_done, h2_full_done = map(sem, ("xn2_done", "t2_done", "h2_full_done"))

        w_in = [sem(f"w_in{i}") for i in range(3 * CHUNKS)]
        w_hi_done, w_lo_dve, w_lo_pool = map(sem, ("w_hi_done", "w_lo_dve", "w_lo_pool"))
        h2_in, h2_hi_done, h2_lo_done = map(sem, ("h2_in", "h2_hi_done", "h2_lo_done"))
        gate_done, up_done, silu_done, h_done, abs_done = map(sem, (
            "gate_done", "up_done", "silu_done", "h_done", "abs_done"))
        mask_step, kept_done, hs_hi_done, hs_lo_done, down_done = map(sem, (
            "mask_step", "kept_done", "hs_hi_done", "hs_lo_done", "down_done"))
        y_in, y_scaled, y_done, y_out = map(sem, ("y_in", "y_scaled", "y_done", "y_out"))

        block = ctx.enter_context(nc.Block())

        def w_dram(c, m):
            cols = slice(c * CH, (c + 1) * CH)
            if m == 2:
                return w_down[cols, :].rearrange("(p j) d -> p j d", j=J)
            return (w_gate, w_up)[m].rearrange("(k p) i -> p k i", p=P)[:, :, cols]

        def w_stage(c, m):
            return y if (c, m) == (1, 1) else w_raw[:].rearrange("p (a b) -> p a b", b=CH)

        def w_split_views(c, m):
            hi, lo = (gate_w, up_w, down_w)[m][c % SLOTS]
            raw = w_stage(c, m)
            if m < 2:
                raw = raw.rearrange("q k (p j) -> q k j p", j=J)
            return hi, lo, raw

        SPLITS = [(0, 0), (0, 1), (1, 0), (1, 1), (0, 2), (1, 2),
                  (2, 0), (2, 1), (3, 0), (3, 1), (2, 2), (3, 2)]
        RANK = {cm: i for i, cm in enumerate(SPLITS)}
        DVE_SPLITS = 4

        def w_lo_wait(eng, cm):
            if RANK[cm] < DVE_SPLITS:
                eng.wait_ge(w_lo_dve, RANK[cm] + 1)
            else:
                eng.wait_ge(w_lo_pool, RANK[cm] + 1 - DVE_SPLITS)

        def place(t):
            return (t + 1) % X_RING

        @block.sync
        def _(sp):
            with nc.allow_non_contiguous_dma(reason="16-byte rows of small tables"):
                sp.dma_start(cT_sb[:], cT.rearrange("(k p) b -> p k b", p=P)).then_inc(small_in, 16)
                wmod_k = wmod.rearrange("(k p) (i n) -> p i k n", p=P, n=D)
                for i, block_ in enumerate((SA, CA)):
                    sp.dma_start(wmod_sb[:, i], wmod_k[:, block_]).then_inc(wmod1_in, 16)
                sp.dma_start(x_ring[:, place(0)], x_t[0]).then_inc(x_in[place(0)], 16)
                sp.dma_start(banks_r[0][:].rearrange("p a b c -> p a (b c)"),
                             wqT.rearrange("(k p) n -> p k n", p=P)).then_inc(wq_in, 16)
                sp.dma_start(norm_raw[:], norm_hd.rearrange("(k p) n -> p k n", p=P)).then_inc(norm_in, 16)
                sp.dma_start(mem_raw[:], mem_hd.rearrange("(k p) n e -> p k n e", p=P)).then_inc(norm_in, 16)
                sp.dma_start(bank_sb[:], bank_w.partition_broadcast(P)).then_inc(norm_in, 16)
                for i, block_ in enumerate((GA, GB)):
                    sp.dma_start(x_ring[:, place(2 - i)], wmod_k[:, block_]).then_inc(wmod_gates_in, 16)
                sp.dma_start(h2_full[:], woT.rearrange("(k p) n -> p k n", p=P)).then_inc(wo_in, 16)
                sp.wait_ge(mods_mm, 1)
                for i, block_ in enumerate((SB, CB)):
                    sp.dma_start(wmod_sb[:, i], wmod_k[:, block_]).then_inc(wmod2_in, 16)
                sp.wait_ge(gates_mm, 2)
                for t in (1, 2):
                    sp.dma_start(x_ring[:, place(t)], x_t[t]).then_inc(x_in[place(t)], 16)
            sp.wait_ge(gates_ready, 1)
            sp.dma_start(gate_dram.rearrange("g b d -> b g d"), gates[:]).then_inc(gates_out, 16)
            sp.wait_ge(gates_out, 16)
            for b in range(B):
                sp.dma_start(ga_all[:, b], gate_dram[0, b].partition_broadcast(P)).then_inc(ga_in, 16)

            def store_x1(t):
                sp.wait_ge(x1_done, 4 * t + 4)
                sp.dma_start(x1_t[t], x_ring[:, place(t)]).then_inc(x1_out, 16)

            def store_h2(t):
                sp.wait_ge(h2_full_done, 4 * t + 4)
                sp.dma_start(h2_dram[t].rearrange("p (k n) -> p k n", k=K), h2_full[:]).then_inc(h2_out, 16)

            def load_w(cm):
                sp.dma_start(w_stage(*cm), w_dram(*cm)).then_inc(w_in[RANK[cm]], 16)

            for t in range(1, NT):
                store_x1(t - 1)
                if t + 2 < NT:
                    sp.wait_ge(xn2_done, 4 * t)
                    sp.wait_ge(x1_out, 16 * t)
                    sp.dma_start(x_ring[:, place(t + 2)], x_t[t + 2]).then_inc(x_in[place(t + 2)], 16)
                if t == 1:
                    load_w((0, 0))
                if t == NT - 1:
                    sp.wait_ge(sigma_done, 4 * NT)
                    sp.wait_ge(x1_out, 16 * t)
                    sp.dma_start(h2_raw[:], h2_dram[0].rearrange("p (k n) -> p k n", k=K)).then_inc(h2_in, 16)
                    sp.wait_ge(w_lo_dve, 1)
                    load_w((0, 1))
                store_h2(t - 1)
            sp.wait_ge(w_lo_dve, 2)
            load_w((1, 0))
            store_x1(NT - 1)
            store_h2(NT - 1)
            sp.wait_ge(x1_out, 16 * NT)
            sp.wait_ge(h2_out, 16 * NT)

            def load_h2(t2):
                sp.dma_start(h2_raw[:], h2_dram[t2].rearrange("p (k n) -> p k n", k=K)).then_inc(h2_in, 16)

            load_w((1, 1))
            sp.wait_ge(w_lo_dve, 3)
            load_w((0, 2))
            sp.wait_ge(h2_lo_done, 4)
            load_h2(1)
            sp.wait_ge(w_lo_pool, 1)
            load_w((1, 2))
            sp.wait_ge(w_lo_dve, 4)

            def load_y(src, tile):
                sp.dma_start(y, src[tile]).then_inc(y_in, 16)
                sp.dma_start(gb_row, gate_dram[1, tile // TB].partition_broadcast(P)).then_inc(y_in, 16)

            def store_y(dst, tile, t2):
                sp.wait_ge(y_done, 4 * t2 + 4)
                sp.dma_start(dst[tile], y).then_inc(y_out, 16)
                sp.wait_ge(y_out, 16 * (t2 + 1))

            load_y(x1_t, 0)
            with sp.Fori(1, NT - 1) as t:
                sp.wait_ge(h2_lo_done, 4 * t + 4)
                load_h2(t + 1)
                store_y(acc_t, t - 1, t - 1)
                load_y(x1_t, t)
            t = NT - 1
            sp.wait_ge(w_lo_pool, 2)
            load_w(SPLITS[6])
            sp.wait_ge(h2_lo_done, 4 * t + 4)
            load_h2(0)
            sp.wait_ge(w_lo_pool, 3)
            load_w(SPLITS[7])
            store_y(acc_t, t - 1, t - 1)
            load_y(x1_t, t)
            for i in (8, 9, 10):
                sp.wait_ge(w_lo_pool, i - DVE_SPLITS)
                load_w(SPLITS[i])
            t = NT
            sp.wait_ge(h2_lo_done, 4 * t + 4)
            load_h2(1)
            sp.wait_ge(w_lo_pool, 11 - DVE_SPLITS)
            load_w(SPLITS[11])
            store_y(acc_t, NT - 1, t - 1)
            load_y(acc_t, 0)
            with sp.Fori(NT + 1, NT2 - 1) as t:
                sp.wait_ge(h2_lo_done, 4 * t + 4)
                sp.dma_start(h2_raw[:], h2_dram[t - NT + 1].rearrange("p (k n) -> p k n", k=K)).then_inc(h2_in, 16)
                store_y(out_t, t - NT - 1, t - 1)
                load_y(acc_t, t - NT)
            t = NT2 - 1
            store_y(out_t, NT - 2, t - 1)
            load_y(acc_t, NT - 1)
            store_y(out_t, NT - 1, t)

        @block.gpsimd
        def _(pool):
            nc.gpsimd.memset(ident[:], 0.0).then_inc(ident_zero, 1)
            pool.wait_ge(ident_zero, 1)
            nc.gpsimd.affine_select(out=ident[:], in_=ident[:], compare_op=ALU.not_equal, fill=1.0, base=0,
                                    pattern=[[-1, P]], channel_multiplier=1).then_inc(ident_ready, 1)
            pool.wait_ge(wa_hi, 3)
            nc.gpsimd.tensor_tensor(wo_lo[:], h2_full[:], wo_hi[:].bitcast(F32), ALU.subtract).then_inc(wa_lo, 1)

            def sigma_low(t):
                for g in range(K):
                    pool.wait_ge(sigma_hi_done, 4 * t + g + 1)
                    nc.gpsimd.tensor_tensor(sigma_lo[:, g], sigma[:, g], sigma_hi[:, g].bitcast(F32),
                                            ALU.subtract).then_inc(sigma_lo_done, 1)

            def tile(t, first=False, last=False):
                for s in range(S):
                    u = 4 * t + s
                    r = banks_r[s % 2]
                    pool.wait_ge(banks_r_done, 4 * u + 4)
                    nc.gpsimd.tensor_tensor(r[:, :, 0:2], r[:, :, 0:2], r[:, :, 2:4],
                                            ALU.add).then_inc(half_sum_done, 1)
                    pool.wait_ge(half_sum_done, u + 1)
                    if not (first and s == 0):
                        pool.wait_ge(combT_done, u)
                    nc.gpsimd.tensor_tensor(combined[:], r[:, :, 0], r[:, :, 1],
                                            ALU.add).then_inc(comb_done, 1)
                if not last:
                    sigma_low(t + 1)

            sigma_low(0)
            tile(0, first=True)
            with pool.Fori(1, NT - 1) as t:
                tile(t)
            tile(NT - 1, last=True)

            def split_w(cm):
                hi, lo, raw = w_split_views(*cm)
                pool.wait_ge(w_hi_done, RANK[cm] + 1)
                nc.gpsimd.tensor_tensor(lo[:], raw, hi[:].bitcast(F32), ALU.subtract).then_inc(w_lo_pool, 1)

            def h2_low(t2):
                for k in range(K):
                    pool.wait_ge(h2_hi_done, 4 * t2 + k + 1)
                    nc.gpsimd.tensor_tensor(h2_lo[:, k], h2_raw[:, k], h2_hi[:, k].bitcast(F32),
                                            ALU.subtract).then_inc(h2_lo_done, 1)

            def hs_low(n):
                for j in range(J):
                    pool.wait_ge(hs_hi_done, 4 * n + j + 1)
                    nc.gpsimd.tensor_tensor(hs_lo[:, j], h_abs[:, j], hs_hi[:, j].bitcast(F32),
                                            ALU.subtract).then_inc(hs_lo_done, 1)

            def tile_b(t2, last=False):
                hs_low(2 * t2 - 1)
                hs_low(2 * t2)
                if not last:
                    h2_low(t2 + 1)

            h2_low(0)
            hs_low(0)
            split_w(SPLITS[4])
            split_w(SPLITS[5])
            h2_low(1)
            with pool.Fori(1, NT - 1) as t2:
                tile_b(t2)
            t2 = NT - 1
            hs_low(2 * t2 - 1)
            split_w(SPLITS[6])
            hs_low(2 * t2)
            split_w(SPLITS[7])
            h2_low(t2 + 1)
            t2 = NT
            hs_low(2 * t2 - 1)
            split_w(SPLITS[8])
            split_w(SPLITS[9])
            hs_low(2 * t2)
            split_w(SPLITS[10])
            h2_low(t2 + 1)
            split_w(SPLITS[11])
            with pool.Fori(NT + 1, NT2 - 1) as t2:
                tile_b(t2)
            tile_b(NT2 - 1, last=True)
            hs_low(2 * NT2 - 1)

        @block.scalar
        def _(act):
            act.wait_ge(small_in, 16)
            nc.scalar.activation(silu_c[:], cT_sb[:], ACT.Silu).then_inc(silu_c_ready, 1)

            def normalize(t, which, dst, done):
                act.wait_ge(shift_done[which], t + 1)
                for s in range(S):
                    nc.scalar.activation(dst[:, s], x_ring[:, place(t), s], ACT.Identity,
                                         bias=ln_shift[:, which, s:s + 1],
                                         scale=ln_rstd[:, which, s:s + 1]).then_inc(done, 1)

            def ln_sqrt(t, which):
                act.wait_ge(var_done[which], t + 1)
                nc.scalar.activation(ln_sd[:, which], ln_var[:, which], ACT.Sqrt).then_inc(sd_done[which], 1)

            def h1_split(t, first=False, between=lambda: None):
                def full(k):
                    act.wait_ge(t1_done, 4 * t + k + 1)
                    if not (first and k < 2):
                        act.wait_ge(h1_lo_done, 4 * t + k - 1)
                    b = t // TB
                    nc.scalar.activation(h1_full[:, k % 2], bank[6 + k % 2][:], ACT.Identity,
                                         bias=mods[:, 0, k, bass.ds(b, 1)] if not first else mods[:, 0, k, 0:1],
                                         scale=mods[:, 1, k, bass.ds(b, 1)] if not first else mods[:, 1, k, 0:1]
                                         ).then_inc(h1_full_done, 1)

                def hi(k):
                    act.wait_ge(h1_full_done, 4 * t + k + 1)
                    nc.scalar.activation(h1_hi[:, k], h1_full[:, k % 2], ACT.Copy).then_inc(h1_hi_done, 1)

                full(0)
                full(1)
                if not first:
                    act.wait_ge(q_done, 4 * t)
                hi(0)
                hi(1)
                between()
                full(2)
                hi(2)
                full(3)
                hi(3)

            def h2_affine(t, first=False, blocks=range(K)):
                b = t // TB
                for k in blocks:
                    act.wait_ge(t2_done, 4 * t + k + 1)
                    if k == 0 and not first:
                        act.wait_ge(h2_out, 16 * t)
                    nc.scalar.activation(h2_full[:, k], bank[6 + k % 2][:], ACT.Identity,
                                         bias=mods[:, 2, k, bass.ds(b, 1)],
                                         scale=mods[:, 3, k, bass.ds(b, 1)]).then_inc(h2_full_done, 1)

            def sigma_exp(t, g, first=False):
                act.wait_ge(q_done, 4 * t + g + 1)
                if not (first and g < 2):
                    act.wait_ge(sigma_done, 4 * t + g - 1)
                nc.scalar.activation(exp_q[:, g % 2], bank[g][:], ACT.Relu, scale=-1.0).then_inc(neg_done, 1)
                act.wait_ge(neg_done, 4 * t + g + 1)
                nc.scalar.activation(exp_q[:, g % 2], exp_q[:, g % 2], ACT.Exp, scale=-1.0).then_inc(exp_done, 1)

            def sigma_high(t, g):
                act.wait_ge(sigma_done, 4 * t + g + 1)
                nc.scalar.activation(sigma_hi[:, g], sigma[:, g], ACT.Copy).then_inc(sigma_hi_done, 1)

            def sigma_all(t, first=False):
                sigma_exp(t, 0, first)
                sigma_exp(t, 1, first)
                sigma_high(t, 0)
                sigma_exp(t, 2)
                sigma_high(t, 1)
                sigma_exp(t, 3)
                sigma_high(t, 2)
                sigma_high(t, 3)

            def combT_high(u, par, warm=True):
                act.wait_ge(combT_done, u + 1)
                if warm:
                    act.wait_ge(wo_done, u - 1)
                nc.scalar.activation(combT_hi[par][:].rearrange("p k n -> p (k n)"), bank[5][:],
                                     ACT.Copy).then_inc(combT_hi_done, 1)

            act.wait_ge(wq_in, 16)
            nc.scalar.activation(wq_hi[:], banks_r[0][:].rearrange("p a b c -> p a (b c)"),
                                 ACT.Copy).then_inc(wa_hi, 1)
            act.wait_ge(bank_shifted, 1)
            nc.scalar.activation(bank_sb[:], bank_sb[:], ACT.Exp).then_inc(bank_exp, 1)
            ln_sqrt(0, 0)
            normalize(0, 0, xn1, xn1_done)
            act.wait_ge(mods_ready, 1)
            h1_split(0, first=True)
            act.wait_ge(mem_bd_ready, 1)
            nc.scalar.activation(mem_hi[:], xn2[:], ACT.Copy).then_inc(wa_hi, 1)
            act.wait_ge(wo_in, 16)
            nc.scalar.activation(wo_hi[:], h2_full[:], ACT.Copy).then_inc(wa_hi, 1)
            sigma_all(0, first=True)

            def tile(t, first=False, last=False):
                for s in range(S):
                    u = 4 * t + s

                    def transposed():
                        if not (first and s == 0):
                            combT_high(u - 1, (s - 1) % 2, warm=not (first and s <= 2))

                    if s == 0:
                        transposed()
                    if s == 1:
                        if not last:
                            ln_sqrt(t + 1, 0)
                            normalize(t + 1, 0, xn1, xn1_done)
                        transposed()
                    if s == 2:
                        if not first:
                            ln_sqrt(t - 1, 1)
                        if not last:
                            h1_split(t + 1)
                        if not first:
                            normalize(t - 1, 1, xn2, xn2_done)
                        transposed()
                    if s == 3:
                        if not first:
                            h2_affine(t - 1)
                        transposed()
                    if last and s < 2:
                        split_w(SPLITS[s])
                if last:
                    h2_high(0)
                else:
                    sigma_all(t + 1)

            def split_w(cm):
                hi, _, raw = w_split_views(*cm)
                act.wait_ge(w_in[RANK[cm]], 16)
                nc.scalar.activation(hi[:], raw, ACT.Copy).then_inc(w_hi_done, 1)

            def h2_high(t2):
                act.wait_ge(h2_in, 16 * (t2 + 1))
                for k in range(K):
                    nc.scalar.activation(h2_hi[:, k], h2_raw[:, k], ACT.Copy).then_inc(h2_hi_done, 1)

            tile(0, first=True)
            act.wait_ge(wa_lo, 1)
            act.wait_ge(mods_ready, 2)
            with act.Fori(1, NT - 1) as t:
                tile(t)
            tile(NT - 1, last=True)
            combT_high(4 * NT - 1, 1)

            def hs_high(n, first=False):
                if not first:
                    act.wait_ge(down_done, 4 * n)
                for j in range(J):
                    act.wait_ge(kept_done, 4 * n + j + 1)
                    nc.scalar.activation(hs_hi[:, j], h_abs[:, j], ACT.Copy).then_inc(hs_hi_done, 1)

            def silu(n, j, first=False):
                act.wait_ge(gate_done, 4 * n + j + 1)
                if not (first and j < 2):
                    act.wait_ge(h_done, 4 * n + j - 1)
                nc.scalar.activation(silu_g[:, j % 2], bank[2 * (j % 2)][:], ACT.Silu).then_inc(silu_done, 1)

            def absolute(n, cc, j, first=False):
                act.wait_ge(h_done, 4 * n + j + 1)
                if not first:
                    act.wait_ge(hs_lo_done, 4 * n - 4 + j + 1)
                nc.scalar.activation(h_abs[:, j], h_act[:, cc, j], ACT.Abs).then_inc(abs_done, 1)

            def item(n, cc, between={}):
                silu(n, 0)
                for j in range(J):
                    if j + 1 < J:
                        silu(n, j + 1)
                    absolute(n, cc, j)
                    if j in between:
                        between[j]()

            def tile_b(t2, last=False):
                hs_high(2 * t2 - 1)
                item(2 * t2, 0)
                hs_high(2 * t2)
                item(2 * t2 + 1, 1)
                if not last:
                    act.wait_ge(up_done, 8 * t2 + 8)
                    h2_high(t2 + 1)

            last_tile = NT - 1
            silu(0, 0, first=True)
            ln_sqrt(last_tile, 1)
            silu(0, 1, first=True)
            normalize(last_tile, 1, xn2, xn2_done)
            absolute(0, 0, 0, first=True)
            silu(0, 2)
            absolute(0, 0, 1, first=True)
            h2_affine(last_tile, blocks=(0, 1))
            silu(0, 3)
            absolute(0, 0, 2, first=True)
            h2_affine(last_tile, blocks=(2, 3))
            absolute(0, 0, 3, first=True)
            act.wait_ge(x1_out, 16 * NT)
            act.wait_ge(h2_out, 16 * NT)
            split_w(SPLITS[2])
            split_w(SPLITS[3])
            hs_high(0, first=True)
            split_w(SPLITS[4])
            item(1, 1, {0: lambda: split_w(SPLITS[5])})
            act.wait_ge(up_done, 8)
            h2_high(1)
            with act.Fori(1, NT - 1) as t2:
                tile_b(t2)
            t2 = NT - 1
            hs_high(2 * t2 - 1)
            item(2 * t2, 0)
            act.wait_ge(up_done, 8 * t2 + 4)
            split_w(SPLITS[6])
            hs_high(2 * t2)
            item(2 * t2 + 1, 1, {2: lambda: split_w(SPLITS[7])})
            act.wait_ge(up_done, 8 * t2 + 8)
            h2_high(t2 + 1)
            t2 = NT
            hs_high(2 * t2 - 1)
            item(2 * t2, 0, {0: lambda: split_w(SPLITS[8]), 2: lambda: split_w(SPLITS[9])})
            hs_high(2 * t2)
            item(2 * t2 + 1, 1, {0: lambda: split_w(SPLITS[10])})
            act.wait_ge(up_done, 8 * t2 + 8)
            h2_high(t2 + 1)
            act.wait_ge(down_done, 4 * (2 * t2))
            split_w(SPLITS[11])
            with act.Fori(NT + 1, NT2 - 1) as t2:
                tile_b(t2)
            tile_b(NT2 - 1, last=True)
            hs_high(2 * NT2 - 1)

        @block.vector
        def _(dve):
            chain = [0]

            def link(ins):
                chain[0] += 1
                ins.then_inc(setup_dve, 1)
                dve.wait_ge(setup_dve, chain[0])

            def ln_stats(t, which, s, done):
                nc.vector.bn_stats(ln_raw[:, which, s], x_ring[:, place(t), s]).then_inc(done, 1)

            def ln_aggregate(t, which, ag):
                for s in range(S):
                    nc.vector.bn_aggr(ln_mv[:, which, s], ln_raw[:, which, s]).then_inc(ag, 1)
                dve.wait_ge(ag, 4 * t + 4)

            def ln_variance(which):
                ins = nc.vector.tensor_scalar(ln_var[:, which], ln_mv[:, which, :, 1], LN_EPS, None, ALU.add)
                ins.then_inc(var_done[which], 1)

            def ln_scalars(t, which):
                dve.wait_ge(sd_done[which], t + 1)
                nc.vector.reciprocal(ln_rstd[:, which], ln_sd[:, which]).then_inc(rstd_done[which], 1)
                dve.wait_ge(rstd_done[which], t + 1)
                nc.vector.scalar_tensor_tensor(out=ln_shift[:, which], in0=ln_mv[:, which, :, 0], scalar=-1.0,
                                               in1=ln_rstd[:, which], op0=ALU.mult,
                                               op1=ALU.mult).then_inc(shift_done[which], 1)

            def h1_low(t, blocks=range(K)):
                for k in blocks:
                    dve.wait_ge(h1_hi_done, 4 * t + k + 1)
                    nc.vector.tensor_tensor(h1_lo[:, k], h1_full[:, k % 2], h1_hi[:, k].bitcast(F32),
                                            ALU.subtract).then_inc(h1_lo_done, 1)

            def sigma_of(t):
                for g in range(K):
                    dve.wait_ge(exp_done, 4 * t + g + 1)
                    nc.vector.scalar_tensor_tensor(out=sigma[:, g], in0=bank[g][:], scalar=0.0,
                                                   in1=exp_q[:, g % 2], op0=ALU.max,
                                                   op1=ALU.add).then_inc(sigma_done, 1)

            nc.vector.memset(ones[:], 1.0).then_inc(consts_ready, 1)
            nc.vector.memset(xn2[:], 0.0)
            link(nc.vector.memset(norm_bd[:], 0.0))
            dve.wait_ge(x_in[place(0)], 16)
            for s in range(S):
                ln_stats(0, 0, s, bn1_done)
            dve.wait_ge(bn1_done, 4)
            ln_aggregate(0, 0, ag1_done)
            ln_variance(0)
            dve.wait_ge(wa_hi, 1)
            nc.vector.tensor_tensor(wq_lo[:], banks_r[0][:].rearrange("p a b c -> p a (b c)"),
                                    wq_hi[:].bitcast(F32), ALU.subtract)
            dve.wait_ge(norm_in, 48)
            link(nc.vector.tensor_reduce(bank_red[:], bank_sb[:], AX_X, ALU.max))
            nc.vector.tensor_tensor(bank_sb[:], bank_sb[:], bank_red[:].unsqueeze(2).broadcast_to([P, K * HG, NB]),
                                    ALU.subtract).then_inc(bank_shifted, 1)
            ln_scalars(0, 0)
            mem_bd = xn2[:].rearrange("p k (n h e) -> p k n h e", n=NB, h=HG)
            for hh in range(HG):
                rows = slice(DH * hh, DH * hh + DH)
                for k in range(K):
                    nc.vector.tensor_copy(mem_bd[rows, k, :, hh, :], mem_raw[rows, k])
                ins = nc.vector.tensor_copy(norm_bd[rows, :, :, hh], norm_raw[rows])
            ins.then_inc(mem_bd_ready, 1)
            dve.wait_ge(mods_mm, 1)
            mm = bank[7][:, 0:4 * K * B].rearrange("p (i k b) -> p i k b", i=4, k=K)
            nc.vector.tensor_copy(mods[:, 0], mm[:, 0])
            nc.vector.tensor_scalar(mods[:, 1], mm[:, 1], 1.0, None, ALU.add).then_inc(mods_ready, 1)
            h1_low(0)
            dve.wait_ge(bank_exp, 1)
            link(nc.vector.tensor_reduce(bank_red[:], bank_sb[:], AX_X, ALU.add))
            link(nc.vector.reciprocal(bank_red[:], bank_red[:]))
            link(nc.vector.tensor_tensor(bank_sb[:], bank_sb[:],
                                         bank_red[:].unsqueeze(2).broadcast_to([P, K * HG, NB]), ALU.mult))
            dve.wait_ge(active_mm, 1)
            link(nc.vector.tensor_reduce(active_sum[:],
                                         bank[5][:, 0:K * NB].rearrange("p (k n) -> p n k", k=K), AX_X, ALU.add))
            link(nc.vector.tensor_scalar(active_sum[:], active_sum[:], NORM_EPS, None, ALU.is_ge))
            for k in range(K):
                ins = nc.vector.tensor_tensor(bank_gate[:, k],
                                              bank_sb[:, HG * k:HG * k + HG].rearrange("p h n -> p n h"),
                                              active_sum[:].unsqueeze(2).broadcast_to([P, NB, HG]), ALU.mult)
            link(ins)
            dve.wait_ge(wa_hi, 2)
            nc.vector.tensor_tensor(mem_lo[:], xn2[:], mem_hi[:].bitcast(F32), ALU.subtract).then_inc(gate_ready, 1)
            sigma_of(0)
            dve.wait_ge(mods_mm, 2)
            nc.vector.tensor_copy(mods[:, 2], mm[:, 2])
            nc.vector.tensor_scalar(mods[:, 3], mm[:, 3], 1.0, None, ALU.add).then_inc(mods_ready, 1)
            dve.wait_ge(gates_mm, 2)
            gate_abs = banks_r[0][0:B, 0:2].rearrange("b i n c -> b i (n c)")
            for i in range(2):
                nc.vector.tensor_copy(gates[:, i], bank[3 + i][0:B, :]).then_inc(setup_dve, 1)
            chain[0] += 2
            dve.wait_ge(setup_dve, chain[0])
            link(nc.vector.scalar_tensor_tensor(out=gate_abs, in0=gates[:], scalar=-1.0, in1=gates[:],
                                                op0=ALU.mult, op1=ALU.max))
            link(nc.vector.tensor_scalar(gate_abs, gate_abs, 0.25, None, ALU.max))
            link(nc.vector.tensor_scalar(gates[:], gates[:], 0.0, 2.0, ALU.is_ge, ALU.mult))
            nc.vector.scalar_tensor_tensor(out=gates[:], in0=gates[:], scalar=-1.0, in1=gate_abs,
                                           op0=ALU.add, op1=ALU.mult).then_inc(gates_ready, 1)

            def attn_rest(tp, sp_, u):
                dve.wait_ge(wo_done, u + 1)
                b = tp // TB
                nc.vector.tensor_tensor(attn_scaled[:], bank[4][:], ga_all[:, b], ALU.mult
                                        ).then_inc(attn_scaled_done, 1)
                dve.wait_ge(attn_scaled_done, u + 1)
                xs = x_ring[:, place(tp), sp_]
                nc.vector.tensor_tensor(xs, xs, attn_scaled[:], ALU.add).then_inc(x1_done, 1)
                dve.wait_ge(x1_done, u + 1)
                ln_stats(tp, 1, sp_, bn2_done)

            def combT_low(u, par):
                dve.wait_ge(combT_hi_done, u + 1)
                nc.vector.tensor_tensor(combT_lo[par][:].rearrange("p k n -> p (k n)"), bank[5][:],
                                        combT_hi[par][:].rearrange("p k n -> p (k n)").bitcast(F32),
                                        ALU.subtract).then_inc(combT_lo_done, 1)

            def split_w_low(cm):
                hi, lo, raw = w_split_views(*cm)
                dve.wait_ge(w_hi_done, RANK[cm] + 1)
                nc.vector.tensor_tensor(lo[:], raw, hi[:].bitcast(F32), ALU.subtract).then_inc(w_lo_dve, 1)

            def scale_banks(u, s, first=False):
                inv = inv_norm[:, s % 2]
                dve.wait_ge(norm_done, u + 1)
                if not (first and s < 2):
                    dve.wait_ge(comb_done, u - 1)
                nc.vector.tensor_scalar(inv, bank[6][:, 0:K * NB * HG], NORM_EPS, None,
                                        ALU.max).then_inc(clip_done, 1)
                dve.wait_ge(clip_done, u + 1)
                nc.vector.reciprocal(inv, inv).then_inc(recip_done, 1)
                dve.wait_ge(recip_done, u + 1)
                nc.vector.tensor_tensor(inv, inv, bank_gate[:].rearrange("p k n h -> p (k n h)"),
                                        ALU.mult).then_inc(r_done, 1)
                dve.wait_ge(r_done, u + 1)
                for g in range(K):
                    dve.wait_ge(banks_done, 4 * u + g + 1)
                    r = inv[:, g * NB * HG:(g + 1) * NB * HG]
                    nc.vector.tensor_tensor(
                        banks_r[s % 2][:, g].rearrange("p n (h e) -> p (n h) e", h=HG),
                        bank[g][:].rearrange("p (a e) -> p a e", e=DH),
                        r.unsqueeze(2).broadcast_to([P, NB * HG, DH]), ALU.mult).then_inc(banks_r_done, 1)

            def tile(t, x_wait=None, first=False, last=False):
                u = 4 * t
                if not last:
                    x_wait()
                    for s in range(S):
                        ln_stats(t + 1, 0, s, bn1_done)
                if not first:
                    attn_rest(t - 1, 2, u - 2)
                    if not last:
                        dve.wait_ge(bn1_done, 4 * t + 8)
                    combT_low(u - 1, 1)
                scale_banks(u, 0, first)
                if not last:
                    if first:
                        dve.wait_ge(bn1_done, 8)
                    ln_aggregate(t + 1, 0, ag1_done)
                    ln_variance(0)
                scale_banks(u + 1, 1, first)
                if not last:
                    ln_scalars(t + 1, 0)
                if not first:
                    attn_rest(t - 1, 3, u - 1)
                    dve.wait_ge(bn2_done, 4 * t)
                combT_low(u, 0)
                if not first:
                    ln_aggregate(t - 1, 1, ag2_done)
                    ln_variance(1)
                if last:
                    split_w_low(SPLITS[0])
                scale_banks(u + 2, 0, first)
                if not first:
                    ln_scalars(t - 1, 1)
                if not last:
                    h1_low(t + 1, (0, 1))
                if first:
                    dve.wait_ge(ga_in, 16 * B)
                attn_rest(t, 0, u)
                if not last:
                    h1_low(t + 1, (2, 3))
                combT_low(u + 1, 1)
                if last:
                    split_w_low(SPLITS[1])
                scale_banks(u + 3, 1, first)
                attn_rest(t, 1, u + 1)
                combT_low(u + 2, 0)
                if not last:
                    sigma_of(t + 1)

            tile(0, lambda: dve.wait_ge(x_in[place(1)], 16), first=True)
            with dve.Fori(0, (NT - 2) // X_RING) as r:
                for i in range(X_RING):
                    nxt = 2 + i
                    fills = r + (1 + nxt // X_RING)
                    tile(r * X_RING + (1 + i), lambda: dve.wait_ge(x_in[place(nxt)], fills * 16))
            tile(NT - 1, last=True)

            def hidden_act(n, cc, j):
                dve.wait_ge(silu_done, 4 * n + j + 1)
                dve.wait_ge(up_done, 4 * n + j + 1)
                nc.vector.tensor_tensor(h_act[:, cc, j], bank[2 * (j % 2) + 1][:], silu_g[:, j % 2],
                                        ALU.mult).then_inc(h_done, 1)

            MASK_STEPS = 10

            def sparsify(n, cc):
                def step(ins):
                    ins.then_inc(mask_step, 1)

                def done(i):
                    dve.wait_ge(mask_step, MASK_STEPS * n + i)

                even, odd = h_abs[:, 0:J:2], h_abs[:, 1:J:2]
                dve.wait_ge(abs_done, 4 * n + 4)
                step(nc.vector.tensor_tensor(pair_hi[:], even, odd, ALU.max))
                step(nc.vector.tensor_tensor(pair_lo[:], even, odd, ALU.min))
                step(nc.vector.tensor_tensor(first_wins[:], even, odd, ALU.is_ge))
                done(2)
                step(nc.vector.tensor_tensor(both_of[:, 0], pair_lo[:, 0], pair_hi[:, 1], ALU.is_ge))
                step(nc.vector.tensor_tensor(both_of[:, 1], pair_lo[:, 1], pair_hi[:, 0], ALU.is_gt))
                done(5)
                step(nc.vector.tensor_tensor(one_each[:, 0], both_of[:, 0], both_of[:, 1], ALU.is_equal))
                done(6)
                step(nc.vector.tensor_tensor(first_wins[:], first_wins[:],
                                             one_each[:].broadcast_to([P, 2, T]), ALU.mult))
                done(7)
                step(nc.vector.tensor_tensor(keep[:, 0:J:2], both_of[:], first_wins[:], ALU.add))
                step(nc.vector.tensor_tensor(keep[:, 1], both_of[:, 1], first_wins[:, 0], ALU.is_equal))
                step(nc.vector.tensor_tensor(keep[:, 3], both_of[:, 0], first_wins[:, 1], ALU.is_equal))
                done(10)
                for j in range(J):
                    nc.vector.tensor_tensor(h_abs[:, j], keep[:, j], h_act[:, cc, j],
                                            ALU.mult).then_inc(kept_done, 1)

            def add_ffn(t2):
                dve.wait_ge(y_in, 32 * (t2 + 1))
                for s in range(S):
                    dve.wait_ge(down_done, 4 * (2 * t2 + 1) + s + 1)
                    nc.vector.tensor_tensor(ffn_scaled[:, s % 2], bank[4 + s][:], gb_row,
                                            ALU.mult).then_inc(y_scaled, 1)
                    dve.wait_ge(y_scaled, 4 * t2 + s + 1)
                    nc.vector.tensor_tensor(y[:, s], y[:, s], ffn_scaled[:, s % 2], ALU.add).then_inc(y_done, 1)

            def tile_b(t2, first=False):
                for cc in range(SLOTS):
                    n = 2 * t2 + cc
                    if not (first and cc == 0):
                        for j in range(J):
                            hidden_act(n, cc, j)
                            if cc == 1 and j == 1 and not first:
                                add_ffn(t2 - 1)
                    sparsify(n, cc)

            attn_rest(NT - 1, 2, 4 * NT - 2)
            combT_low(4 * NT - 1, 1)
            hidden_act(0, 0, 0)
            attn_rest(NT - 1, 3, 4 * NT - 1)
            dve.wait_ge(bn2_done, 4 * NT)
            ln_aggregate(NT - 1, 1, ag2_done)
            ln_variance(1)
            hidden_act(0, 0, 1)
            ln_scalars(NT - 1, 1)
            hidden_act(0, 0, 2)
            hidden_act(0, 0, 3)
            split_w_low(SPLITS[2])
            split_w_low(SPLITS[3])
            tile_b(0, first=True)
            with dve.Fori(1, NT2) as t2:
                tile_b(t2)
            add_ffn(NT2 - 1)

        @block.tensor
        def _(pe):
            def mm3(out_, stat, mov, start, stop):
                nc.tensor.matmul(out_, stat[0], mov[0], start=start, stop=False)
                nc.tensor.matmul(out_, stat[0], mov[1], start=False, stop=False)
                return nc.tensor.matmul(out_, stat[1], mov[0], start=False, stop=stop)

            def mod_scalars(i, at_block):
                for f in range(K):
                    for k in range(K):
                        at = (i * K + f) * B
                        ins = nc.tensor.matmul(bank[7][:, at:at + B],
                                               wmod_sb[:, at_block, k, f * P:(f + 1) * P], silu_c[:, k],
                                               start=(k == 0), stop=(k == K - 1))
                return ins

            pe.wait_ge(silu_c_ready, 1)
            pe.wait_ge(wmod1_in, 32)
            mod_scalars(0, 0)
            mod_scalars(1, 1).then_inc(mods_mm, 1)

            def ln_transpose(src, t, k, done):
                for s in range(S):
                    ins = nc.tensor.transpose(bank[6 + k % 2][:, s * P:(s + 1) * P], src[:, s, k * P:(k + 1) * P],
                                              ident[:])
                ins.then_inc(done, 1)

            def t1(t, k):
                if k == 0:
                    pe.wait_ge(xn1_done, 4 * t + 4)
                if k >= 2:
                    pe.wait_ge(h1_full_done, 4 * t + k - 1)
                ln_transpose(xn1, t, k, t1_done)

            def t2(t, k):
                if k == 0:
                    pe.wait_ge(xn2_done, 4 * t + 4)
                if k >= 2:
                    pe.wait_ge(h2_full_done, 4 * t + k - 1)
                ln_transpose(xn2, t, k, t2_done)

            def q_block(t, g, first=False):
                if not first:
                    pe.wait_ge(banks_r_done, 4 * (4 * t - 1) + g + 1)
                for k in range(K):
                    if g == 0:
                        pe.wait_ge(h1_lo_done, 4 * t + k + 1)
                    ins = mm3(bank[g][:], (wq_hi[:, k, g * P:(g + 1) * P], wq_lo[:, k, g * P:(g + 1) * P]),
                              (h1_hi[:, k], h1_lo[:, k]), k == 0, k == K - 1)
                ins.then_inc(q_done, 1)

            def norms(u, s):
                for g in range(K):
                    cols = slice(g * NB * HG, (g + 1) * NB * HG)
                    ins = nc.tensor.matmul(bank[6][:, cols], sigma[:, g, s * P:(s + 1) * P],
                                           norm_bd[:, g].rearrange("p n h -> p (n h)"), start=True, stop=True)
                ins.then_inc(norm_done, 1)

            def banks_of(t, s):
                u = 4 * t + s
                for g in range(K):
                    if s == 0:
                        pe.wait_ge(sigma_lo_done, 4 * t + g + 1)
                    else:
                        pe.wait_ge(banks_r_done, 4 * u - 3 + g)
                    mm3(bank[g][:], (sigma_hi[:, g, s * P:(s + 1) * P], sigma_lo[:, g, s * P:(s + 1) * P]),
                        (mem_hi[:, g], mem_lo[:, g]), True, True).then_inc(banks_done, 1)

            def comb_transpose(u, first=False):
                pe.wait_ge(comb_done, u + 1)
                if not first:
                    pe.wait_ge(combT_lo_done, u)
                for g in range(K):
                    ins = nc.tensor.transpose(bank[5][:, g * P:(g + 1) * P], combined[:, g], ident[:])
                ins.then_inc(combT_done, 1)

            def wo_product(u, par, first=False):
                pe.wait_ge(combT_lo_done, u + 1)
                if not first:
                    pe.wait_ge(attn_scaled_done, u)
                for g in range(K):
                    ins = mm3(bank[4][:], (combT_hi[par][:, g], combT_lo[par][:, g]),
                              (wo_hi[:, g], wo_lo[:, g]), g == 0, g == K - 1)
                ins.then_inc(wo_done, 1)

            pe.wait_ge(ident_ready, 1)
            for k in range(K):
                if k == 1:
                    pe.wait_ge(mods_ready, 1)
                t1(0, k)
            pe.wait_ge(consts_ready, 1)
            pe.wait_ge(norm_in, 48)
            nc.tensor.matmul(bank[5][:, 0:K * NB], ones[:], norm_raw[:].rearrange("p k n -> p (k n)"),
                             start=True, stop=True).then_inc(active_mm, 1)
            pe.wait_ge(wa_hi, 1)
            for g in range(K):
                q_block(0, g, first=True)
            pe.wait_ge(sigma_done, 4)
            pe.wait_ge(wmod2_in, 32)
            mod_scalars(2, 0)
            mod_scalars(3, 1).then_inc(mods_mm, 1)
            pe.wait_ge(wmod_gates_in, 32)
            for i, staged in enumerate((place(2), place(1))):
                for k in range(K):
                    ins = nc.tensor.matmul(bank[3 + i][0:B, :], silu_c[:, k], x_ring[:, staged, k],
                                           start=(k == 0), stop=(k == K - 1))
                ins.then_inc(gates_mm, 1)
            pe.wait_ge(gates_ready, 1)
            pe.wait_ge(mods_ready, 2)
            pe.wait_ge(gate_ready, 1)
            pe.wait_ge(wa_lo, 1)

            def tile(t, first=False, last=False):
                u = 4 * t
                if not first:
                    wo_product(u - 2, 0)
                    comb_transpose(u - 1)
                pe.wait_ge(sigma_done, 4 * t + 4)
                norms(u, 0)
                banks_of(t, 0)
                pe.wait_ge(clip_done, u + 1)
                norms(u + 1, 1)
                banks_of(t, 1)
                if not first:
                    wo_product(u - 1, 1)
                comb_transpose(u, first=first)
                pe.wait_ge(clip_done, u + 2)
                norms(u + 2, 2)
                banks_of(t, 2)
                if not last:
                    pe.wait_ge(clip_done, u + 3)
                    t1(t + 1, 0)
                    t1(t + 1, 1)
                wo_product(u, 0, first=first)
                if not last:
                    t1(t + 1, 2)
                    t1(t + 1, 3)
                comb_transpose(u + 1)
                if last:
                    pe.wait_ge(clip_done, u + 3)
                else:
                    pe.wait_ge(h1_full_done, 4 * (t + 1) + 3)
                norms(u + 3, 3)
                banks_of(t, 3)
                if not first:
                    pe.wait_ge(clip_done, u + 4)
                    t2(t - 1, 0)
                    if not last:
                        pe.wait_ge(h1_full_done, 4 * (t + 1) + 4)
                    t2(t - 1, 1)
                wo_product(u + 1, 1)
                if not first:
                    t2(t - 1, 2)
                    t2(t - 1, 3)
                comb_transpose(u + 2)
                if not last:
                    for g in range(K):
                        q_block(t + 1, g)

            tile(0, first=True)
            with pe.Fori(1, NT - 1) as t:
                tile(t)
            tile(NT - 1, last=True)

            def gate_up_block(t2, cc, chunk, j, first=False):
                n = 2 * t2 + cc
                for m, (hi, lo) in enumerate((gate_w[cc], up_w[cc])):
                    if j == 0:
                        w_lo_wait(pe, (chunk, m))
                    if not (first and j < 2):
                        pe.wait_ge((silu_done, h_done)[m], 4 * n + j - 1)
                    for k in range(K):
                        if cc == 0 and j == 0 and m == 0:
                            pe.wait_ge(h2_lo_done, 4 * t2 + k + 1)
                        ins = mm3(bank[2 * (j % 2) + m][:], (hi[:, k, j], lo[:, k, j]),
                                  (h2_hi[:, k], h2_lo[:, k]), k == 0, k == K - 1)
                    ins.then_inc((gate_done, up_done)[m], 1)

            def gate_up(t2, cc, chunk):
                for j in range(J):
                    gate_up_block(t2, cc, chunk, j)

            def down(t2, cc, chunk, first=False):
                n = 2 * t2 + cc
                w_lo_wait(pe, (chunk, 2))
                if cc == 0 and first:
                    pe.wait_ge(attn_scaled_done, 4 * NT)
                    pe.wait_ge(h2_full_done, 4 * NT)
                elif cc == 0:
                    pe.wait_ge(y_scaled, 4 * t2)
                for s in range(S):
                    for j in range(J):
                        if s == 0:
                            pe.wait_ge(hs_lo_done, 4 * n + j + 1)
                        cols = slice(s * P, (s + 1) * P)
                        ins = mm3(bank[4 + s][:], (hs_hi[:, j, cols], hs_lo[:, j, cols]),
                                  (down_w[cc][0][:, j], down_w[cc][1][:, j]),
                                  cc == 0 and j == 0, cc == SLOTS - 1 and j == J - 1)
                    ins.then_inc(down_done, 1)

            def tile_b(t2, pass_, prev_pass):
                gate_up(t2, 0, 2 * pass_)
                down(t2 - 1, 1, 2 * prev_pass + 1)
                gate_up(t2, 1, 2 * pass_ + 1)
                down(t2, 0, 2 * pass_)

            wo_product(4 * NT - 2, 0)
            comb_transpose(4 * NT - 1)
            gate_up_block(0, 0, 0, 0, first=True)
            wo_product(4 * NT - 1, 1)
            gate_up_block(0, 0, 0, 1, first=True)
            gate_up_block(0, 0, 0, 2)
            t2(NT - 1, 0)
            t2(NT - 1, 1)
            gate_up_block(0, 0, 0, 3)
            t2(NT - 1, 2)
            t2(NT - 1, 3)
            gate_up(0, 1, 1)
            down(0, 0, 0, first=True)
            with pe.Fori(1, NT) as t2_:
                tile_b(t2_, 0, 0)
            tile_b(NT, 1, 0)
            with pe.Fori(NT + 1, NT2) as t2_:
                tile_b(t2_, 1, 1)
            down(NT2 - 1, 1, CHUNKS - 1)


_INS = ["x", "wqT", "woT", "bank_w", "mem_hd", "norm_hd", "w_gate", "w_up", "w_down", "cT", "wmod"]


def kernel(**inputs):
    import numpy as _np
    import concourse.bacc as _bacc
    from concourse import mybir as _mybir
    from concourse.bass_utils import run_bass_kernel_spmd as _run

    a = {n: _np.asarray(v) for n, v in inputs.items()}
    x = a["L0_attn_hidden_states"]
    b, s, d = x.shape
    mem, norm = a["L0_attn_memories"], a["L0_attn_memory_norms"]
    nb, h, dh, _ = mem.shape
    laid = {
        "x": x.reshape(b * s, d),
        "wqT": a["L0_attn_Wq"].T,
        "woT": a["L0_attn_Wo"].T,
        "bank_w": a["L0_attn_bank_weights"],
        "mem_hd": mem.transpose(1, 2, 0, 3).reshape(h * dh, nb, dh),
        "norm_hd": norm.transpose(1, 2, 0).reshape(h * dh, nb),
        "w_gate": a["L0_ffn_w_gate"],
        "w_up": a["L0_ffn_w_up"],
        "w_down": a["L0_ffn_w_down"],
        "cT": a["L0_c"].T,
        "wmod": a["L0_wmod"],
    }
    nc = _bacc.Bacc("TRN2", target_bir_lowering=False, num_devices=1)
    arrays, args = {}, []
    for name in _INS:
        v = _np.ascontiguousarray(laid[name])
        arrays[f"in_{name}_dram"] = v
        args.append(nc.dram_tensor(f"in_{name}_dram", v.shape, _mybir.dt.from_np(v.dtype), kind="ExternalInput").ap())
    out = nc.dram_tensor("out_dram", (b * s, d), _mybir.dt.float32, kind="ExternalOutput").ap()
    adaln_kernel(nc, *args, out)
    r = _run(nc, [arrays], core_ids=[0])
    return r.results[0]["out_dram"].reshape(b, s, d)
```

```python
from contextlib import ExitStack

import concourse.bass as bass
from concourse import mybir

F32 = mybir.dt.float32
F32R = mybir.dt.float32r
BF16 = mybir.dt.bfloat16
ALU = mybir.AluOpType
ACT = mybir.ActivationFunctionType
AX_X = mybir.AxisListType.X

P = 128
D = 512
T = 512
S = T // P
SLOTS = 2
K = D // P
B = 4
NB = 4
DH = 32
HG = P // DH
HALF = P // 2
PAIR = 2
J = 4
CH = 512
LN_EPS = 1e-5
NORM_EPS = 1e-6
X_RING = 3
SA, CA, GA, SB, CB, GB = range(6)


def adaln_kernel(nc, x, wqT, woT, bank_w, mem_hd, norm_hd, w_gate, w_up, w_down, cT, wmod, out):
    tokens = x.shape[0]
    NT = tokens // T
    TB = NT // B
    hidden = w_gate.shape[1]
    CHUNKS = hidden // CH
    PASSES = CHUNKS // SLOTS
    NT2 = NT * PASSES

    x1_dram = nc.dram_tensor("x1_scratch", (tokens, D), F32, kind="Internal").ap()
    acc_dram = nc.dram_tensor("acc_scratch", (tokens, D), F32, kind="Internal").ap()
    h2_dram = nc.dram_tensor("h2T_scratch", (NT, P, K * T), F32, kind="Internal").ap()
    gate_dram = nc.dram_tensor("gates_scratch", (2, B, D), F32, kind="Internal").ap()

    def tiled(dram):
        return dram.rearrange("(t p s) d -> t p s d", p=P, s=S)

    x_t, x1_t, acc_t, out_t = tiled(x), tiled(x1_dram), tiled(acc_dram), tiled(out)

    with ExitStack() as ctx:
        def sem(name):
            return ctx.enter_context(nc.semaphore(name))

        bank = [ctx.enter_context(nc.psum_tensor(f"bank{i}", [P, 512], F32)) for i in range(8)]

        w_raw = ctx.enter_context(nc.sbuf_tensor("w_raw", [P, K * CH], F32))

        with ExitStack() as phase_a:
            def sba(name, shape, dt=F32):
                return phase_a.enter_context(nc.sbuf_tensor(name, shape, dt))

            wq_hi = sba("wq_hi", [P, K, D], F32R)
            wq_lo = sba("wq_lo", [P, K, D], F32R)
            h1_hi = sba("h1_hi", [P, K, T], F32R)
            h1_lo = sba("h1_lo", [P, K, T], F32R)
            xn1 = sba("xn1", [P, S, D])
            h1_full = sba("h1_full", [P, K, T])
            exp_q = sba("exp_q", [P, 2, T])
            x_ring = sba("x_ring", [P, X_RING, S, D])
            sigma = sba("sigma", [P, K, T])
            sigma_st = sba("sigma_st", [P, 2 * K, T], F32R)
            mem_hi = sba("mem_hi", [P, K, NB * P], F32R)
            mem_lo = sba("mem_lo", [P, K, NB * P], F32R)
            banks_r0 = sba("banks_r0", [P, K, NB, P])
            with ExitStack() as setup_only:
                wmod_sb = setup_only.enter_context(nc.sbuf_tensor("wmod_sb", [P, 2, K, D], F32))
            banks_r = [banks_r0, sba("banks_r1", [P, K, NB, P])]
            combT_hi = [sba(f"combT_hi{i}", [P, K, P], F32R) for i in range(2)]
            combT_lo = [sba(f"combT_lo{i}", [P, K, P], F32R) for i in range(2)]
            combined = sba("combined", [P, K, P])
            attn_scaled = sba("attn_scaled", [P, D])
            wo_hi = sba("wo_hi", [P, K, D], F32R)
            wo_lo = sba("wo_lo", [P, K, D], F32R)
            ga_all = sba("ga_all", [P, B, D])
            mem_raw = sba("mem_raw", [P, K, NB, DH])
            xn2 = sba("xn2", [P, S, D])
            h2_full = sba("h2_full", [P, K, T])
            ident = sba("ident", [P, P])
            ones = sba("ones", [P, P])
            mem_swapped = sba("mem_swapped", [P, K, NB, DH])
            norm_raw = sba("norm_raw", [P, K, NB])
            norm_bd = sba("norm_bd", [P, K, NB, HG])
            bank_sb = sba("bank_sb", [P, K * HG, NB])
            bank_red = sba("bank_red", [P, K * HG])
            active_sum = sba("active_sum", [P, NB])
            bank_gate = sba("bank_gate", [P, K, NB, HG])
            inv_norm = sba("inv_norm", [P, 2, K * NB * HG])
            cT_sb = sba("cT_sb", [P, K, B])
            silu_c = sba("silu_c", [P, K, B])
            mods = sba("mods", [P, 4, K, B])
            gates = sba("gates", [B, 2, D])
            gate_sign = sba("gate_sign", [B, 2, D])
            mod_rows = gate_sign
            ln_raw = sba("ln_raw", [P, 2, S, 6])
            ln_mv = sba("ln_mv", [P, 2, S, 2])
            ln_var = sba("ln_var", [P, 2, S])
            ln_sd = sba("ln_sd", [P, 2, S])
            ln_rstd = sba("ln_rstd", [P, 2, S])
            ln_shift = sba("ln_shift", [P, 2, S])

        def sbb(name, shape, dt=F32):
            return ctx.enter_context(nc.sbuf_tensor(name, shape, dt))

        def in_halves(name, shape):
            return [sbb(f"{name}_hi", shape, F32R), sbb(f"{name}_lo", shape, F32R)]

        gate_w, up_w, down_w = [None] * SLOTS, [None] * SLOTS, [None] * SLOTS
        gate_w[0] = in_halves("gate_w0", [P, K, J, P])
        up_w[0] = in_halves("up_w0", [P, K, J, P])
        h2_raw = sbb("h2_raw", [P, K, T])
        h2_hi = sbb("h2_hi", [P, K, T], F32R)
        h2_lo = sbb("h2_lo", [P, K, T], F32R)
        silu_g = sbb("silu_g", [P, 2, T])
        over_x1 = sbb("over_x1", [P, 2, S, D])
        h_act = sbb("h_act", [P, SLOTS, J, T])
        h_abs = sbb("h_abs", [P, J, T])
        pair_hi = sbb("pair_hi", [P, 2, T])
        pair_lo = sbb("pair_lo", [P, 2, T])
        first_wins = sbb("first_wins", [P, 2, T], BF16)
        both_of = sbb("both_of", [P, 2, T], BF16)
        one_each = sbb("one_each", [P, 1, T], BF16)
        keep = sbb("keep", [P, J, T], BF16)
        hs_hi = sbb("hs_hi", [P, J, T], F32R)
        hs_lo = sbb("hs_lo", [P, J, T], F32R)
        y = over_x1[:, 0]
        over_x1_rest = over_x1[:, 1]
        gb_row = over_x1_rest[:, 0]
        ffn_scaled = over_x1_rest[:, 1:3]
        gate_w[1] = in_halves("gate_w1", [P, K, J, P])
        up_w[1] = in_halves("up_w1", [P, K, J, P])
        down_w[0] = in_halves("down_w0", [P, J, D])
        down_w[1] = in_halves("down_w1", [P, J, D])

        small_in, norm_in, wq_in, wo_in = map(sem, ("small_in", "norm_in", "wq_in", "wo_in"))
        wmod_in = [sem(f"wmod_in{i}") for i in range(6)]
        x_in = [sem(f"x_in{i}") for i in range(X_RING)]
        gates_out, ga_in, x1_out, h2_out = map(sem, ("gates_out", "ga_in", "x1_out", "h2_out"))
        ident_zero, ident_ready, consts_ready, setup_dve = map(sem, (
            "ident_zero", "ident_ready", "consts_ready", "setup_dve"))
        silu_c_ready, mods_mm, rows_mm, rows_done, gates_mm, active_mm, mods_ready, gates_ready = map(sem, (
            "silu_c_ready", "mods_mm", "rows_mm", "rows_done", "gates_mm", "active_mm", "mods_ready", "gates_ready"))
        gate_sign_done, gate_abs_done = map(sem, ("gate_sign_done", "gate_abs_done"))
        bank_shifted, bank_exp, mem_bd_ready, wa_hi, wa_lo, gate_ready = map(sem, (
            "bank_shifted", "bank_exp", "mem_bd_ready", "wa_hi", "wa_lo", "gate_ready"))
        bn1_done, ag1_done, bn2_done, ag2_done = map(sem, ("bn1_done", "ag1_done", "bn2_done", "ag2_done"))
        var_done, sd_done, rstd_done, shift_done = (
            [sem(f"{name}{i + 1}") for i in range(2)] for name in ("var_done", "sd_done", "rstd_done", "shift_done"))
        xn1_done, t1_done, h1_full_done, h1_hi_done, h1_lo_done = map(sem, (
            "xn1_done", "t1_done", "h1_full_done", "h1_hi_done", "h1_lo_done"))
        q_done, exp_done, neg_done, sigma_done, sigma_hi_done, sigma_lo_done = map(sem, (
            "q_done", "exp_done", "neg_done", "sigma_done", "sigma_hi_done", "sigma_lo_done"))
        sigma_lo_dve = sem("sigma_lo_dve")
        norm_done, clip_done, recip_done, r_done = map(sem, ("norm_done", "clip_done", "recip_done", "r_done"))
        banks_done, banks_r_done, half_sum_done, comb_done = map(sem, (
            "banks_done", "banks_r_done", "half_sum_done", "comb_done"))
        combT_done, combT_hi_done, combT_lo_done = map(sem, ("combT_done", "combT_hi_done", "combT_lo_done"))
        wo_done, attn_scaled_done, x1_done = map(sem, ("wo_done", "attn_scaled_done", "x1_done"))
        xn2_done, t2_done, h2_full_done = map(sem, ("xn2_done", "t2_done", "h2_full_done"))

        w_in = [sem(f"w_in{i}") for i in range(3 * CHUNKS)]
        w_hi_done, w_lo_dve, w_lo_pool = map(sem, ("w_hi_done", "w_lo_dve", "w_lo_pool"))
        h2_in, h2_hi_done, h2_lo_done = map(sem, ("h2_in", "h2_hi_done", "h2_lo_done"))
        gate_done, up_done, silu_done, h_done, abs_done = map(sem, (
            "gate_done", "up_done", "silu_done", "h_done", "abs_done"))
        mask_step, kept_done, hs_hi_done, hs_lo_done, down_done = map(sem, (
            "mask_step", "kept_done", "hs_hi_done", "hs_lo_done", "down_done"))
        y_in, y_scaled, y_done, y_out = map(sem, ("y_in", "y_scaled", "y_done", "y_out"))

        block = ctx.enter_context(nc.Block())

        def w_dram(c, m):
            cols = slice(c * CH, (c + 1) * CH)
            if m == 2:
                return w_down[cols, :].rearrange("(p j) d -> p j d", j=J)
            return (w_gate, w_up)[m].rearrange("(k p) i -> p k i", p=P)[:, :, cols]

        def w_stage(c, m):
            return y if (c, m) == (1, 1) else w_raw[:].rearrange("p (a b) -> p a b", b=CH)

        def w_split_views(c, m):
            hi, lo = (gate_w, up_w, down_w)[m][c % SLOTS]
            raw = w_stage(c, m)
            if m < 2:
                raw = raw.rearrange("q k (p j) -> q k j p", j=J)
            return hi, lo, raw

        SPLITS = [(0, 0), (0, 1), (1, 0), (1, 1), (0, 2), (1, 2),
                  (2, 0), (2, 1), (3, 0), (3, 1), (2, 2), (3, 2)]
        RANK = {cm: i for i, cm in enumerate(SPLITS)}
        DVE_SPLITS = 4

        def w_lo_wait(eng, cm):
            if RANK[cm] < DVE_SPLITS:
                eng.wait_ge(w_lo_dve, RANK[cm] + 1)
            else:
                eng.wait_ge(w_lo_pool, RANK[cm] + 1 - DVE_SPLITS)

        def place(t):
            return (t + 1) % X_RING

        @block.sync
        def _(sp):
            with nc.allow_non_contiguous_dma(reason="16-byte rows of small tables"):
                sp.dma_start(cT_sb[:], cT.rearrange("(k p) b -> p k b", p=P)).then_inc(small_in, 16)
                wmod_k = wmod.rearrange("(k p) (i n) -> p i k n", p=P, n=D)

                def load_mod(block_, place_):
                    sp.dma_start(place_, wmod_k[:, block_]).then_inc(wmod_in[block_], 16)

                load_mod(SA, wmod_sb[:, 0])
                sp.dma_start(x_ring[:, place(0)], x_t[0]).then_inc(x_in[place(0)], 16)
                load_mod(CA, wmod_sb[:, 1])
                sp.dma_start(norm_raw[:], norm_hd.rearrange("(k p) n -> p k n", p=P)).then_inc(norm_in, 16)
                sp.dma_start(mem_raw[:], mem_hd.rearrange("(k p) n e -> p k n e", p=P)).then_inc(norm_in, 16)
                for half in range(2):
                    sp.dma_start(mem_swapped[HALF * (1 - half):HALF * (2 - half)],
                                 mem_hd.rearrange("(k p) n e -> p k n e", p=P)[HALF * half:HALF * (half + 1)]
                                 ).then_inc(norm_in, 16)
                sp.dma_start(bank_sb[:], bank_w.partition_broadcast(P)).then_inc(norm_in, 16)
                sp.dma_start(banks_r[0][:].rearrange("p a b c -> p a (b c)"),
                             wqT.rearrange("(k p) n -> p k n", p=P)).then_inc(wq_in, 16)
                load_mod(GA, x_ring[:, place(2)])
                sp.dma_start(h2_full[:], woT.rearrange("(k p) n -> p k n", p=P)).then_inc(wo_in, 16)
                sp.dma_start(x_ring[:, place(1)], x_t[1]).then_inc(x_in[place(1)], 16)
                sp.wait_ge(mods_mm, 1)
                load_mod(GB, wmod_sb[:, 0])
                sp.wait_ge(gate_ready, 1)
                load_mod(SB, xn2[:])
                sp.wait_ge(gates_mm, 2)
                sp.dma_start(x_ring[:, place(2)], x_t[2]).then_inc(x_in[place(2)], 16)
            sp.wait_ge(gates_ready, 1)
            sp.dma_start(gate_dram.rearrange("g b d -> b g d"), gates[:]).then_inc(gates_out, 16)
            sp.wait_ge(gates_out, 16)
            for b in range(B):
                sp.dma_start(ga_all[:, b], gate_dram[0, b].partition_broadcast(P)).then_inc(ga_in, 16)
            sp.wait_ge(wa_lo, 1)
            load_mod(CB, h2_full[:])

            def store_x1(t):
                sp.wait_ge(x1_done, 4 * t + 4)
                sp.dma_start(x1_t[t], x_ring[:, place(t)]).then_inc(x1_out, 16)

            def store_h2(t):
                sp.wait_ge(h2_full_done, 4 * t + 4)
                sp.dma_start(h2_dram[t].rearrange("p (k n) -> p k n", k=K), h2_full[:]).then_inc(h2_out, 16)

            def load_w(cm):
                sp.dma_start(w_stage(*cm), w_dram(*cm)).then_inc(w_in[RANK[cm]], 16)

            for t in range(1, NT):
                if t == NT - 1:
                    sp.wait_ge(sigma_done, 4 * NT)
                    sp.wait_ge(x1_out, 16 * (t - 1))
                    sp.dma_start(h2_raw[:], h2_dram[0].rearrange("p (k n) -> p k n", k=K)).then_inc(h2_in, 16)
                store_x1(t - 1)
                if t + 2 < NT:
                    sp.wait_ge(xn2_done, 4 * t)
                    sp.wait_ge(x1_out, 16 * t)
                    sp.dma_start(x_ring[:, place(t + 2)], x_t[t + 2]).then_inc(x_in[place(t + 2)], 16)
                if t == 1:
                    load_w((0, 0))
                if t == NT - 1:
                    sp.wait_ge(w_lo_dve, 1)
                    load_w((0, 1))
                    sp.wait_ge(xn2_done, 4 * t)
                    sp.wait_ge(x1_out, 16 * t)
                    load_w((1, 1))
                store_h2(t - 1)
            sp.wait_ge(w_lo_dve, 2)
            load_w((1, 0))
            store_x1(NT - 1)
            store_h2(NT - 1)

            def load_h2(t2):
                sp.dma_start(h2_raw[:], h2_dram[t2].rearrange("p (k n) -> p k n", k=K)).then_inc(h2_in, 16)

            sp.wait_ge(w_lo_dve, 3)
            load_w((0, 2))
            sp.wait_ge(h2_lo_done, 4)
            load_h2(1)
            sp.wait_ge(w_lo_pool, 1)
            load_w((1, 2))
            sp.wait_ge(w_lo_dve, 4)
            sp.wait_ge(x1_out, 16 * NT)

            def load_y(src, tile):
                sp.dma_start(y, src[tile]).then_inc(y_in, 16)
                sp.dma_start(gb_row, gate_dram[1, tile // TB].partition_broadcast(P)).then_inc(y_in, 16)

            def store_y(dst, tile, t2):
                sp.wait_ge(y_done, 4 * t2 + 4)
                sp.dma_start(dst[tile], y).then_inc(y_out, 16)
                sp.wait_ge(y_out, 16 * (t2 + 1))

            load_y(x1_t, 0)
            with sp.Fori(1, NT - 1) as t:
                sp.wait_ge(h2_lo_done, 4 * t + 4)
                load_h2(t + 1)
                store_y(acc_t, t - 1, t - 1)
                load_y(x1_t, t)
            t = NT - 1
            sp.wait_ge(w_lo_pool, 2)
            load_w(SPLITS[6])
            sp.wait_ge(h2_lo_done, 4 * t + 4)
            load_h2(0)
            sp.wait_ge(w_lo_pool, 3)
            load_w(SPLITS[7])
            store_y(acc_t, t - 1, t - 1)
            load_y(x1_t, t)
            for i in (8, 9, 10):
                sp.wait_ge(w_lo_pool, i - DVE_SPLITS)
                load_w(SPLITS[i])
            t = NT
            sp.wait_ge(h2_lo_done, 4 * t + 4)
            load_h2(1)
            sp.wait_ge(w_lo_pool, 11 - DVE_SPLITS)
            load_w(SPLITS[11])
            store_y(acc_t, NT - 1, t - 1)
            load_y(acc_t, 0)
            with sp.Fori(NT + 1, NT2 - 1) as t:
                sp.wait_ge(h2_lo_done, 4 * t + 4)
                sp.dma_start(h2_raw[:], h2_dram[t - NT + 1].rearrange("p (k n) -> p k n", k=K)).then_inc(h2_in, 16)
                store_y(out_t, t - NT - 1, t - 1)
                load_y(acc_t, t - NT)
            t = NT2 - 1
            store_y(out_t, NT - 2, t - 1)
            load_y(acc_t, NT - 1)
            store_y(out_t, NT - 1, t)

        @block.gpsimd
        def _(pool):
            nc.gpsimd.memset(ident[:], 0.0).then_inc(ident_zero, 1)
            pool.wait_ge(ident_zero, 1)
            nc.gpsimd.affine_select(out=ident[:], in_=ident[:], compare_op=ALU.not_equal, fill=1.0, base=0,
                                    pattern=[[-1, P]], channel_multiplier=1).then_inc(ident_ready, 1)
            def sigma_low(t, first=False):
                if not first:
                    pool.wait_ge(comb_done, 4 * t)
                for g in range(K):
                    pool.wait_ge(sigma_hi_done, 8 * t + 2 * g + 1)
                    nc.gpsimd.tensor_tensor(sigma_st[HALF:, 2 * g], sigma[:HALF, g], sigma_st[:HALF, 2 * g].bitcast(F32),
                                            ALU.subtract).then_inc(sigma_lo_done, 1)
                pool.wait_ge(sigma_lo_done, 4 * t + 4)

            def h1_low(t, blocks):
                for k in blocks:
                    pool.wait_ge(h1_hi_done, 4 * t + k + 1)
                    nc.gpsimd.tensor_tensor(h1_lo[:, k], h1_full[:, k], h1_hi[:, k].bitcast(F32),
                                            ALU.subtract).then_inc(h1_lo_done, 1)

            def h2_low(t2):
                for k in range(K):
                    pool.wait_ge(h2_hi_done, 4 * t2 + k + 1)
                    nc.gpsimd.tensor_tensor(h2_lo[:, k], h2_raw[:, k], h2_hi[:, k].bitcast(F32),
                                            ALU.subtract).then_inc(h2_lo_done, 1)

            def tile(t, first=False, last=False):
                for s in range(S):
                    u = 4 * t + s
                    r = banks_r[s % 2][:].rearrange("p k n c -> p (k n c)").rearrange(
                        "p (b n c) -> p b n c", n=NB, c=HALF)
                    for i in range(2):
                        blocks = slice(i * K, (i + 1) * K)
                        pool.wait_ge(banks_r_done, 4 * u + 2 * i + 2)
                        nc.gpsimd.tensor_tensor(r[:, blocks, 0:2], r[:, blocks, 0:2], r[:, blocks, 2:4],
                                                ALU.add).then_inc(half_sum_done, 1)
                    pool.wait_ge(half_sum_done, 2 * u + 2)
                    if not (first and s == 0):
                        pool.wait_ge(combT_done, u)
                    nc.gpsimd.tensor_tensor(combined[:].rearrange("p k (b c) -> p (k b) c", c=HALF), r[:, :, 0], r[:, :, 1],
                                            ALU.add).then_inc(comb_done, 1)
                    if last and s == 1:
                        h2_low(0)
                    if not last and s in (1, 2):
                        h1_low(t + 1, (2 * s - 2, 2 * s - 1))
                if not last:
                    sigma_low(t + 1)

            sigma_low(0, first=True)
            pool.wait_ge(wa_hi, 3)
            nc.gpsimd.tensor_tensor(wo_lo[:], h2_full[:], wo_hi[:].bitcast(F32), ALU.subtract).then_inc(wa_lo, 1)
            tile(0, first=True)
            with pool.Fori(1, NT - 1) as t:
                tile(t)
            tile(NT - 1, last=True)

            def split_w(cm):
                hi, lo, raw = w_split_views(*cm)
                pool.wait_ge(w_hi_done, RANK[cm] + 1)
                nc.gpsimd.tensor_tensor(lo[:], raw, hi[:].bitcast(F32), ALU.subtract).then_inc(w_lo_pool, 1)

            def hs_low(n):
                for j in range(J):
                    pool.wait_ge(hs_hi_done, 4 * n + j + 1)
                    nc.gpsimd.tensor_tensor(hs_lo[:, j], h_abs[:, j], hs_hi[:, j].bitcast(F32),
                                            ALU.subtract).then_inc(hs_lo_done, 1)

            def tile_b(t2, last=False):
                hs_low(2 * t2 - 1)
                hs_low(2 * t2)
                if not last:
                    h2_low(t2 + 1)

            split_w(SPLITS[4])
            hs_low(0)
            h2_low(1)
            split_w(SPLITS[5])
            with pool.Fori(1, NT - 1) as t2:
                tile_b(t2)
            t2 = NT - 1
            hs_low(2 * t2 - 1)
            split_w(SPLITS[6])
            hs_low(2 * t2)
            split_w(SPLITS[7])
            h2_low(t2 + 1)
            t2 = NT
            hs_low(2 * t2 - 1)
            split_w(SPLITS[8])
            split_w(SPLITS[9])
            hs_low(2 * t2)
            split_w(SPLITS[10])
            h2_low(t2 + 1)
            split_w(SPLITS[11])
            with pool.Fori(NT + 1, NT2 - 1) as t2:
                tile_b(t2)
            tile_b(NT2 - 1, last=True)
            hs_low(2 * NT2 - 1)

        @block.scalar
        def _(act):
            act.wait_ge(small_in, 16)
            nc.scalar.activation(silu_c[:], cT_sb[:], ACT.Silu).then_inc(silu_c_ready, 1)

            def normalize(t, which, dst, done):
                act.wait_ge(shift_done[which], t + 1)
                for s in range(S):
                    nc.scalar.activation(dst[:, s], x_ring[:, place(t), s], ACT.Identity,
                                         bias=ln_shift[:, which, s:s + 1],
                                         scale=ln_rstd[:, which, s:s + 1]).then_inc(done, 1)

            def ln_sqrt(t, which):
                act.wait_ge(var_done[which], t + 1)
                nc.scalar.activation(ln_sd[:, which], ln_var[:, which], ACT.Sqrt).then_inc(sd_done[which], 1)

            def h1_split(t, first=False, before_last=lambda: None):
                def full(k):
                    act.wait_ge(t1_done, 4 * t + k + 1)
                    b = t // TB
                    nc.scalar.activation(h1_full[:, k], bank[6 + k % 2][:], ACT.Identity,
                                         bias=mods[:, 0, k, bass.ds(b, 1)] if not first else mods[:, 0, k, 0:1],
                                         scale=mods[:, 1, k, bass.ds(b, 1)] if not first else mods[:, 1, k, 0:1]
                                         ).then_inc(h1_full_done, 1)

                def hi(k):
                    act.wait_ge(h1_full_done, 4 * t + k + 1)
                    nc.scalar.activation(h1_hi[:, k], h1_full[:, k], ACT.Copy).then_inc(h1_hi_done, 1)

                full(0)
                full(1)
                if not first:
                    act.wait_ge(q_done, 4 * t)
                hi(0)
                hi(1)
                full(2)
                hi(2)
                full(3)
                before_last()
                hi(3)

            def h2_affine(t, first=False, blocks=range(K)):
                b = t // TB
                for k in blocks:
                    act.wait_ge(t2_done, 4 * t + k + 1)
                    if k == 0 and not first:
                        act.wait_ge(h2_out, 16 * t)
                    nc.scalar.activation(h2_full[:, k], bank[6 + k % 2][:], ACT.Identity,
                                         bias=mods[:, 2, k, bass.ds(b, 1)],
                                         scale=mods[:, 3, k, bass.ds(b, 1)]).then_inc(h2_full_done, 1)

            def sigma_exp(t, g, first=False):
                act.wait_ge(q_done, 4 * t + g + 1)
                if not (first and g < 2):
                    act.wait_ge(sigma_done, 4 * t + g - 1)
                nc.scalar.activation(exp_q[:, g % 2], bank[g][:], ACT.Relu, scale=-1.0).then_inc(neg_done, 1)
                act.wait_ge(neg_done, 4 * t + g + 1)
                nc.scalar.activation(exp_q[:, g % 2], exp_q[:, g % 2], ACT.Exp, scale=-1.0).then_inc(exp_done, 1)

            def sigma_high(t, g):
                act.wait_ge(sigma_done, 4 * t + g + 1)
                for i, rows in enumerate((slice(0, HALF), slice(HALF, P))):
                    nc.scalar.activation(sigma_st[rows, 2 * g + i], sigma[rows, g], ACT.Copy).then_inc(sigma_hi_done, 1)

            def sigma_all(t, first=False, between=lambda: None):
                sigma_exp(t, 0, first)
                between()
                sigma_exp(t, 1, first)
                sigma_high(t, 0)
                sigma_exp(t, 2)
                sigma_high(t, 1)
                sigma_exp(t, 3)
                sigma_high(t, 2)
                sigma_high(t, 3)

            def combT_high(u, par, warm=True):
                act.wait_ge(combT_done, u + 1)
                if warm:
                    act.wait_ge(wo_done, u - 1)
                nc.scalar.activation(combT_hi[par][:].rearrange("p k n -> p (k n)"), bank[5][:],
                                     ACT.Copy).then_inc(combT_hi_done, 1)

            ln_sqrt(0, 0)
            normalize(0, 0, xn1, xn1_done)
            act.wait_ge(wq_in, 16)
            nc.scalar.activation(wq_hi[:], banks_r[0][:].rearrange("p a b c -> p a (b c)"),
                                 ACT.Copy).then_inc(wa_hi, 1)
            act.wait_ge(mods_ready, 1)
            h1_split(0, first=True)
            act.wait_ge(mem_bd_ready, 1)
            nc.scalar.activation(mem_hi[:], xn2[:], ACT.Copy).then_inc(wa_hi, 1)
            act.wait_ge(bank_shifted, 1)
            nc.scalar.activation(bank_sb[:], bank_sb[:], ACT.Exp).then_inc(bank_exp, 1)
            sigma_all(0, first=True)
            act.wait_ge(wo_in, 16)
            nc.scalar.activation(wo_hi[:], h2_full[:], ACT.Copy).then_inc(wa_hi, 1)
            for i in range(2):
                act.wait_ge(gate_sign_done, i + 1)
                nc.scalar.activation(gates[:, i], bank[4 + i][0:B, :], ACT.Abs, scale=2.0).then_inc(gate_abs_done, 1)

            def copy_row(i):
                act.wait_ge(gates_ready, 1)
                act.wait_ge(rows_mm, i + 1)
                nc.scalar.activation(mod_rows[:, i], bank[7][0:B, :], ACT.Copy).then_inc(rows_done, 1)

            def tile(t, first=False, last=False):
                for s in range(S):
                    u = 4 * t + s

                    def transposed():
                        if not (first and s == 0):
                            combT_high(u - 1, (s - 1) % 2, warm=not (first and s <= 2))

                    if s == 0:
                        transposed()
                        if not last:
                            ln_sqrt(t + 1, 0)
                            normalize(t + 1, 0, xn1, xn1_done)
                    if first and s in (1, 3):
                        copy_row(s // 2)
                    if s == 1:
                        transposed()
                        if not first:
                            ln_sqrt(t - 1, 1)
                    if s == 2:
                        if last:
                            transposed()
                        else:
                            h1_split(t + 1, before_last=transposed)
                        if not first:
                            normalize(t - 1, 1, xn2, xn2_done)
                    if s == 3:
                        if not first:
                            h2_affine(t - 1, blocks=(0, 1))
                        transposed()
                    if last and s == 0:
                        split_w(SPLITS[0])
                    if last and s == 1:
                        h2_high(0)
                    if last and s == 2:
                        split_w(SPLITS[1])

                def h2_rest():
                    if not first:
                        h2_affine(t - 1, blocks=(2, 3))

                if last:
                    h2_rest()
                else:
                    sigma_all(t + 1, between=h2_rest)

            def split_w(cm):
                hi, _, raw = w_split_views(*cm)
                act.wait_ge(w_in[RANK[cm]], 16)
                nc.scalar.activation(hi[:], raw, ACT.Copy).then_inc(w_hi_done, 1)

            def h2_high(t2):
                act.wait_ge(h2_in, 16 * (t2 + 1))
                for k in range(K):
                    nc.scalar.activation(h2_hi[:, k], h2_raw[:, k], ACT.Copy).then_inc(h2_hi_done, 1)

            tile(0, first=True)
            act.wait_ge(wa_lo, 1)
            act.wait_ge(mods_ready, 2)
            with act.Fori(1, NT - 1) as t:
                tile(t)
            tile(NT - 1, last=True)
            combT_high(4 * NT - 1, 1)

            def hs_high(n, first=False):
                if not first:
                    act.wait_ge(down_done, 4 * n)
                for j in range(J):
                    act.wait_ge(kept_done, 4 * n + j + 1)
                    nc.scalar.activation(hs_hi[:, j], h_abs[:, j], ACT.Copy).then_inc(hs_hi_done, 1)

            def silu(n, j, first=False):
                act.wait_ge(gate_done, 4 * n + j + 1)
                if not (first and j < 2):
                    act.wait_ge(h_done, 4 * n + j - 1)
                nc.scalar.activation(silu_g[:, j % 2], bank[2 * (j % 2)][:], ACT.Silu).then_inc(silu_done, 1)

            def absolute(n, cc, j, first=False):
                act.wait_ge(h_done, 4 * n + j + 1)
                if not first:
                    act.wait_ge(hs_lo_done, 4 * n - 4 + j + 1)
                nc.scalar.activation(h_abs[:, j], h_act[:, cc, j], ACT.Abs).then_inc(abs_done, 1)

            def item(n, cc, between={}, started=False):
                if not started:
                    silu(n, 0)
                for j in range(J):
                    if j + 1 < J:
                        silu(n, j + 1)
                    absolute(n, cc, j)
                    if j in between:
                        between[j]()

            def tile_b(t2, last=False):
                hs_high(2 * t2 - 1)
                item(2 * t2, 0)
                hs_high(2 * t2)
                item(2 * t2 + 1, 1)
                if not last:
                    act.wait_ge(up_done, 8 * t2 + 8)
                    h2_high(t2 + 1)

            last_tile = NT - 1
            silu(0, 0, first=True)
            ln_sqrt(last_tile, 1)
            silu(0, 1, first=True)
            normalize(last_tile, 1, xn2, xn2_done)
            act.wait_ge(x1_done, 4 * NT)
            split_w(SPLITS[2])
            absolute(0, 0, 0, first=True)
            h2_affine(last_tile, blocks=(0, 1))
            silu(0, 2)
            absolute(0, 0, 1, first=True)
            h2_affine(last_tile, blocks=(2, 3))
            split_w(SPLITS[3])
            silu(0, 3)
            absolute(0, 0, 2, first=True)
            absolute(0, 0, 3, first=True)
            act.wait_ge(h2_out, 16 * NT)
            split_w(SPLITS[4])
            silu(1, 0)
            hs_high(0, first=True)
            item(1, 1, started=True)
            act.wait_ge(up_done, 8)
            h2_high(1)
            split_w(SPLITS[5])
            with act.Fori(1, NT - 1) as t2:
                tile_b(t2)
            t2 = NT - 1
            hs_high(2 * t2 - 1)
            item(2 * t2, 0)
            act.wait_ge(up_done, 8 * t2 + 4)
            split_w(SPLITS[6])
            hs_high(2 * t2)
            item(2 * t2 + 1, 1, {2: lambda: split_w(SPLITS[7])})
            act.wait_ge(up_done, 8 * t2 + 8)
            h2_high(t2 + 1)
            t2 = NT
            hs_high(2 * t2 - 1)
            item(2 * t2, 0, {0: lambda: split_w(SPLITS[8]), 2: lambda: split_w(SPLITS[9])})
            hs_high(2 * t2)
            item(2 * t2 + 1, 1, {0: lambda: split_w(SPLITS[10])})
            act.wait_ge(up_done, 8 * t2 + 8)
            h2_high(t2 + 1)
            act.wait_ge(down_done, 4 * (2 * t2))
            split_w(SPLITS[11])
            with act.Fori(NT + 1, NT2 - 1) as t2:
                tile_b(t2)
            tile_b(NT2 - 1, last=True)
            hs_high(2 * NT2 - 1)

        @block.vector
        def _(dve):
            chain = [0]

            def link(ins):
                chain[0] += 1
                ins.then_inc(setup_dve, 1)
                dve.wait_ge(setup_dve, chain[0])

            def ln_stats(t, which, s, done):
                nc.vector.bn_stats(ln_raw[:, which, s], x_ring[:, place(t), s]).then_inc(done, 1)

            def ln_aggregate(t, which, ag):
                for s in range(S):
                    nc.vector.bn_aggr(ln_mv[:, which, s], ln_raw[:, which, s]).then_inc(ag, 1)
                dve.wait_ge(ag, 4 * t + 4)

            def ln_variance(which):
                ins = nc.vector.tensor_scalar(ln_var[:, which], ln_mv[:, which, :, 1], LN_EPS, None, ALU.add)
                ins.then_inc(var_done[which], 1)

            def ln_scalars(t, which):
                dve.wait_ge(sd_done[which], t + 1)
                nc.vector.reciprocal(ln_rstd[:, which], ln_sd[:, which]).then_inc(rstd_done[which], 1)
                dve.wait_ge(rstd_done[which], t + 1)
                nc.vector.scalar_tensor_tensor(out=ln_shift[:, which], in0=ln_mv[:, which, :, 0], scalar=-1.0,
                                               in1=ln_rstd[:, which], op0=ALU.mult,
                                               op1=ALU.mult).then_inc(shift_done[which], 1)

            def h1_low(t):
                for k in range(K):
                    dve.wait_ge(h1_hi_done, 4 * t + k + 1)
                    nc.vector.tensor_tensor(h1_lo[:, k], h1_full[:, k], h1_hi[:, k].bitcast(F32),
                                            ALU.subtract).then_inc(h1_lo_done, 1)

            def sigma_of(t, g):
                dve.wait_ge(exp_done, 4 * t + g + 1)
                nc.vector.scalar_tensor_tensor(out=sigma[:, g], in0=bank[g][:], scalar=0.0, in1=exp_q[:, g % 2],
                                               op0=ALU.max, op1=ALU.add).then_inc(sigma_done, 1)

            def sigma_low(t, g):
                dve.wait_ge(sigma_hi_done, 8 * t + 2 * g + 2)
                nc.vector.tensor_tensor(sigma_st[:HALF, 2 * g + 1], sigma[HALF:, g],
                                        sigma_st[HALF:, 2 * g + 1].bitcast(F32),
                                        ALU.subtract).then_inc(sigma_lo_dve, 1)

            nc.vector.memset(ones[:], 1.0).then_inc(consts_ready, 1)
            nc.vector.memset(xn2[:], 0.0)
            link(nc.vector.memset(norm_bd[:], 0.0))
            dve.wait_ge(x_in[place(0)], 16)
            for s in range(S):
                ln_stats(0, 0, s, bn1_done)
            dve.wait_ge(bn1_done, 4)
            ln_aggregate(0, 0, ag1_done)
            ln_variance(0)
            ln_scalars(0, 0)
            dve.wait_ge(norm_in, 80)
            link(nc.vector.tensor_reduce(bank_red[:], bank_sb[:], AX_X, ALU.max))
            nc.vector.tensor_tensor(bank_sb[:], bank_sb[:], bank_red[:].unsqueeze(2).broadcast_to([P, K * HG, NB]),
                                    ALU.subtract).then_inc(bank_shifted, 1)
            mem_bd = xn2[:].rearrange("p k (b n h e) -> p k b n h e", b=PAIR, n=NB, h=PAIR)
            norm_cols = norm_bd[:].rearrange("p k n h -> p k (n h)").rearrange(
                "p k (b n h) -> p k b n h", b=PAIR, n=NB)
            for hh in range(HG):
                rows = slice(DH * hh, DH * hh + DH)
                pair, h = hh // PAIR, hh % PAIR
                for k in range(K):
                    nc.vector.tensor_copy(mem_bd[rows, k, pair, :, h, :], mem_raw[rows, k])
                    nc.vector.tensor_copy(mem_bd[rows, k, 1 - pair, :, h, :], mem_swapped[rows, k])
                ins = nc.vector.tensor_copy(norm_cols[rows, :, pair, :, h], norm_raw[rows])
            ins.then_inc(mem_bd_ready, 1)
            dve.wait_ge(wa_hi, 1)
            nc.vector.tensor_tensor(wq_lo[:], banks_r[0][:].rearrange("p a b c -> p a (b c)"),
                                    wq_hi[:].bitcast(F32), ALU.subtract)
            dve.wait_ge(mods_mm, 1)
            mm, mm2 = (bank[i][:, 0:2 * K * B].rearrange("p (i k b) -> p i k b", i=2, k=K) for i in (7, 6))
            nc.vector.tensor_copy(mods[:, 0], mm[:, 0])
            nc.vector.tensor_scalar(mods[:, 1], mm[:, 1], 1.0, None, ALU.add).then_inc(mods_ready, 1)
            h1_low(0)
            dve.wait_ge(bank_exp, 1)
            link(nc.vector.tensor_reduce(bank_red[:], bank_sb[:], AX_X, ALU.add))
            link(nc.vector.reciprocal(bank_red[:], bank_red[:]))
            link(nc.vector.tensor_tensor(bank_sb[:], bank_sb[:],
                                         bank_red[:].unsqueeze(2).broadcast_to([P, K * HG, NB]), ALU.mult))
            dve.wait_ge(active_mm, 1)
            link(nc.vector.tensor_reduce(active_sum[:],
                                         bank[5][:, 0:K * NB].rearrange("p (k n) -> p n k", k=K), AX_X, ALU.add))
            link(nc.vector.tensor_scalar(active_sum[:], active_sum[:], NORM_EPS, None, ALU.is_ge))
            gate_cols = bank_gate[:].rearrange("p k n h -> p (k n h)").rearrange(
                "p (b n h) -> p b n h", n=NB, h=PAIR)
            for pair in range(PAIR * K):
                ins = nc.vector.tensor_tensor(gate_cols[:, pair],
                                              bank_sb[:, PAIR * pair:PAIR * (pair + 1)].rearrange("p h n -> p n h"),
                                              active_sum[:].unsqueeze(2).broadcast_to([P, NB, PAIR]), ALU.mult)
            link(ins)
            dve.wait_ge(wa_hi, 2)
            nc.vector.tensor_tensor(mem_lo[:], xn2[:], mem_hi[:].bitcast(F32), ALU.subtract).then_inc(gate_ready, 1)
            for g in range(K):
                sigma_of(0, g)
                if g > 0:
                    sigma_low(0, g - 1)
            sigma_low(0, K - 1)
            for i in range(2):
                dve.wait_ge(gates_mm, i + 1)
                nc.vector.tensor_scalar(gate_sign[:, i], bank[4 + i][0:B, :], 0.0, 0.5, ALU.is_ge,
                                        ALU.subtract).then_inc(gate_sign_done, 1)
            dve.wait_ge(gate_sign_done, 2)
            dve.wait_ge(gate_abs_done, 2)
            nc.vector.scalar_tensor_tensor(out=gates[:], in0=gates[:], scalar=0.5, in1=gate_sign[:],
                                           op0=ALU.max, op1=ALU.mult).then_inc(gates_ready, 1)

            def attn_rest(tp, sp_, u, between=lambda: None):
                dve.wait_ge(wo_done, u + 1)
                b = tp // TB
                nc.vector.tensor_tensor(attn_scaled[:], bank[4][:], ga_all[:, b], ALU.mult
                                        ).then_inc(attn_scaled_done, 1)
                between()
                dve.wait_ge(attn_scaled_done, u + 1)
                xs = x_ring[:, place(tp), sp_]
                nc.vector.tensor_tensor(xs, xs, attn_scaled[:], ALU.add).then_inc(x1_done, 1)
                dve.wait_ge(x1_done, u + 1)
                ln_stats(tp, 1, sp_, bn2_done)

            def combT_low(u, par):
                dve.wait_ge(combT_hi_done, u + 1)
                nc.vector.tensor_tensor(combT_lo[par][:].rearrange("p k n -> p (k n)"), bank[5][:],
                                        combT_hi[par][:].rearrange("p k n -> p (k n)").bitcast(F32),
                                        ALU.subtract).then_inc(combT_lo_done, 1)

            def split_w_low(cm):
                hi, lo, raw = w_split_views(*cm)
                dve.wait_ge(w_hi_done, RANK[cm] + 1)
                nc.vector.tensor_tensor(lo[:], raw, hi[:].bitcast(F32), ALU.subtract).then_inc(w_lo_dve, 1)

            def scale_banks(u, s, first=False, between=lambda: None):
                inv = inv_norm[:, s % 2]
                dve.wait_ge(norm_done, u + 1)
                if not (first and s < 2):
                    dve.wait_ge(comb_done, u - 1)
                nc.vector.tensor_scalar(inv, bank[6][:, 0:K * NB * HG], NORM_EPS, None,
                                        ALU.max).then_inc(clip_done, 1)
                between()
                dve.wait_ge(clip_done, u + 1)
                nc.vector.reciprocal(inv, inv).then_inc(recip_done, 1)
                dve.wait_ge(recip_done, u + 1)
                nc.vector.tensor_tensor(inv, inv, bank_gate[:].rearrange("p k n h -> p (k n h)"),
                                        ALU.mult).then_inc(r_done, 1)
                dve.wait_ge(r_done, u + 1)
                for g in range(K):
                    dve.wait_ge(banks_done, 4 * u + g + 1)
                    r = inv[:, g * NB * HG:(g + 1) * NB * HG]
                    nc.vector.tensor_tensor(
                        banks_r[s % 2][:, g].rearrange("p n (h e) -> p (n h) e", h=HG),
                        bank[g][:].rearrange("p (a e) -> p a e", e=DH),
                        r.unsqueeze(2).broadcast_to([P, NB * HG, DH]), ALU.mult).then_inc(banks_r_done, 1)

            def tile(t, x_wait=None, first=False, last=False):
                u = 4 * t
                def stats(*subtiles):
                    for s in subtiles:
                        ln_stats(t + 1, 0, s, bn1_done)

                def next_scalars():
                    if not last:
                        ln_scalars(t + 1, 0)

                if first:
                    scale_banks(u, 0, first)
                    x_wait()
                    stats(0, 1, 2, 3)
                    dve.wait_ge(bn1_done, 8)
                    ln_aggregate(t + 1, 0, ag1_done)
                    ln_variance(0)
                elif last:
                    for g in range(K):
                        sigma_of(t, g)
                        if g > 0:
                            sigma_low(t, g - 1)
                    sigma_low(t, K - 1)
                else:
                    sigma_of(t, 0)
                    x_wait()
                    stats(0)
                    sigma_of(t, 1)
                    sigma_low(t, 0)
                    stats(1, 2, 3)
                    dve.wait_ge(bn1_done, 4 * t + 8)
                    sigma_of(t, 2)
                    sigma_low(t, 1)
                    ln_aggregate(t + 1, 0, ag1_done)
                    ln_variance(0)
                    sigma_of(t, 3)
                    sigma_low(t, 2)
                    sigma_low(t, 3)
                if not first:
                    attn_rest(t - 1, 2, u - 2, between=lambda: combT_low(u - 1, 1))
                    scale_banks(u, 0, between=next_scalars)
                scale_banks(u + 1, 1, first, between=next_scalars if first else lambda: None)
                if not first:
                    attn_rest(t - 1, 3, u - 1)
                combT_low(u, 0)
                if last:
                    split_w_low(SPLITS[0])
                def last_variance():
                    if not first:
                        ln_aggregate(t - 1, 1, ag2_done)
                        ln_variance(1)

                if not first:
                    dve.wait_ge(bn2_done, 4 * t)
                scale_banks(u + 2, 0, first, between=last_variance)
                if not first:
                    ln_scalars(t - 1, 1)
                if first:
                    dve.wait_ge(ga_in, 16 * B)
                attn_rest(t, 0, u, between=lambda: combT_low(u + 1, 1))
                scale_banks(u + 3, 1, first)
                attn_rest(t, 1, u + 1, between=lambda: combT_low(u + 2, 0))
                if first:
                    dve.wait_ge(mods_mm, 2)
                    nc.vector.tensor_copy(mods[:, 2], mm2[:, 0])
                    nc.vector.tensor_scalar(mods[:, 3], mm2[:, 1], 1.0, None, ALU.add).then_inc(mods_ready, 1)

            tile(0, lambda: dve.wait_ge(x_in[place(1)], 16), first=True)
            with dve.Fori(0, (NT - 2) // X_RING) as r:
                for i in range(X_RING):
                    nxt = 2 + i
                    fills = r + (1 + nxt // X_RING)
                    tile(r * X_RING + (1 + i), lambda: dve.wait_ge(x_in[place(nxt)], fills * 16))
            tile(NT - 1, last=True)

            def hidden_act(n, cc, j):
                dve.wait_ge(silu_done, 4 * n + j + 1)
                dve.wait_ge(up_done, 4 * n + j + 1)
                nc.vector.tensor_tensor(h_act[:, cc, j], bank[2 * (j % 2) + 1][:], silu_g[:, j % 2],
                                        ALU.mult).then_inc(h_done, 1)

            MASK_STEPS = 10

            def sparsify(n, cc):
                def step(ins):
                    ins.then_inc(mask_step, 1)

                def done(i):
                    dve.wait_ge(mask_step, MASK_STEPS * n + i)

                even, odd = h_abs[:, 0:J:2], h_abs[:, 1:J:2]
                dve.wait_ge(abs_done, 4 * n + 4)
                step(nc.vector.tensor_tensor(pair_hi[:], even, odd, ALU.max))
                step(nc.vector.tensor_tensor(pair_lo[:], even, odd, ALU.min))
                step(nc.vector.tensor_tensor(first_wins[:], even, odd, ALU.is_ge))
                done(2)
                step(nc.vector.tensor_tensor(both_of[:, 0], pair_lo[:, 0], pair_hi[:, 1], ALU.is_ge))
                step(nc.vector.tensor_tensor(both_of[:, 1], pair_lo[:, 1], pair_hi[:, 0], ALU.is_gt))
                done(5)
                step(nc.vector.tensor_tensor(one_each[:, 0], both_of[:, 0], both_of[:, 1], ALU.is_equal))
                done(6)
                step(nc.vector.tensor_tensor(first_wins[:], first_wins[:],
                                             one_each[:].broadcast_to([P, 2, T]), ALU.mult))
                done(7)
                step(nc.vector.tensor_tensor(keep[:, 0:J:2], both_of[:], first_wins[:], ALU.add))
                step(nc.vector.tensor_tensor(keep[:, 1], both_of[:, 1], first_wins[:, 0], ALU.is_equal))
                step(nc.vector.tensor_tensor(keep[:, 3], both_of[:, 0], first_wins[:, 1], ALU.is_equal))
                done(10)
                for j in range(J):
                    nc.vector.tensor_tensor(h_abs[:, j], keep[:, j], h_act[:, cc, j],
                                            ALU.mult).then_inc(kept_done, 1)

            def add_ffn(t2):
                dve.wait_ge(y_in, 32 * (t2 + 1))
                for s in range(S):
                    dve.wait_ge(down_done, 4 * (2 * t2 + 1) + s + 1)
                    nc.vector.tensor_tensor(ffn_scaled[:, s % 2], bank[4 + s][:], gb_row,
                                            ALU.mult).then_inc(y_scaled, 1)
                    dve.wait_ge(y_scaled, 4 * t2 + s + 1)
                    nc.vector.tensor_tensor(y[:, s], y[:, s], ffn_scaled[:, s % 2], ALU.add).then_inc(y_done, 1)

            def tile_b(t2, first=False):
                for cc in range(SLOTS):
                    n = 2 * t2 + cc
                    if not (first and cc == 0):
                        for j in range(J):
                            hidden_act(n, cc, j)
                            if cc == 1 and j == 1 and not first:
                                add_ffn(t2 - 1)
                    sparsify(n, cc)

            split_w_low(SPLITS[1])
            attn_rest(NT - 1, 2, 4 * NT - 2)
            combT_low(4 * NT - 1, 1)
            hidden_act(0, 0, 0)
            attn_rest(NT - 1, 3, 4 * NT - 1)
            dve.wait_ge(bn2_done, 4 * NT)
            ln_aggregate(NT - 1, 1, ag2_done)
            ln_variance(1)
            ln_scalars(NT - 1, 1)
            hidden_act(0, 0, 1)
            split_w_low(SPLITS[2])
            hidden_act(0, 0, 2)
            split_w_low(SPLITS[3])
            hidden_act(0, 0, 3)
            tile_b(0, first=True)
            with dve.Fori(1, NT2) as t2:
                tile_b(t2)
            add_ffn(NT2 - 1)

        @block.tensor
        def _(pe):
            def mm3(out_, stat, mov, start, stop):
                nc.tensor.matmul(out_, stat[0], mov[0], start=start, stop=False)
                nc.tensor.matmul(out_, stat[0], mov[1], start=False, stop=False)
                return nc.tensor.matmul(out_, stat[1], mov[0], start=False, stop=stop)

            def mod_scalars(i, block_):
                pe.wait_ge(wmod_in[block_], 16)
                for f in range(K):
                    for k in range(K):
                        at = (i * K + f) * B
                        ins = nc.tensor.matmul(bank[7][:, at:at + B], wmod_sb[:, i, k, f * P:(f + 1) * P],
                                               silu_c[:, k], start=(k == 0), stop=(k == K - 1))
                return ins

            def mod_row(block_, staged, to):
                pe.wait_ge(wmod_in[block_], 16)
                for k in range(K):
                    ins = nc.tensor.matmul(to[0:B, :], silu_c[:, k], staged[:, k], start=(k == 0), stop=(k == K - 1))
                return ins

            pe.wait_ge(silu_c_ready, 1)
            mod_scalars(0, SA)
            mod_scalars(1, CA).then_inc(mods_mm, 1)

            def ln_transpose(src, t, k, done):
                for s in range(S):
                    ins = nc.tensor.transpose(bank[6 + k % 2][:, s * P:(s + 1) * P], src[:, s, k * P:(k + 1) * P],
                                              ident[:])
                ins.then_inc(done, 1)

            def t1(t, k):
                if k == 0:
                    pe.wait_ge(xn1_done, 4 * t + 4)
                if k >= 2:
                    pe.wait_ge(h1_full_done, 4 * t + k - 1)
                ln_transpose(xn1, t, k, t1_done)

            def t2(t, k):
                if k == 0:
                    pe.wait_ge(xn2_done, 4 * t + 4)
                if k >= 2:
                    pe.wait_ge(h2_full_done, 4 * t + k - 1)
                ln_transpose(xn2, t, k, t2_done)

            def q_block(t, g, first=False):
                if not first:
                    pe.wait_ge(banks_r_done, 4 * (4 * t - 1) + g + 1)
                for k in range(K):
                    if g == 0:
                        pe.wait_ge(h1_lo_done, 4 * t + k + 1)
                    ins = mm3(bank[g][:], (wq_hi[:, k, g * P:(g + 1) * P], wq_lo[:, k, g * P:(g + 1) * P]),
                              (h1_hi[:, k], h1_lo[:, k]), k == 0, k == K - 1)
                ins.then_inc(q_done, 1)

            def norms(u, s):
                for g in range(K):
                    cols = slice(g * NB * HG, (g + 1) * NB * HG)
                    ins = nc.tensor.matmul(bank[6][:, cols], sigma[:, g, s * P:(s + 1) * P],
                                           norm_bd[:, g].rearrange("p n h -> p (n h)"), start=True, stop=True)
                ins.then_inc(norm_done, 1)

            def banks_of(t, s):
                u = 4 * t + s
                for g in range(K):
                    if s == 0:
                        pe.wait_ge(sigma_lo_done, 4 * t + g + 1)
                        pe.wait_ge(sigma_lo_dve, 4 * t + g + 1)
                    else:
                        pe.wait_ge(banks_r_done, 4 * u - 3 + g)
                    for pair in range(PAIR):
                        cols = slice(pair * T // PAIR, (pair + 1) * T // PAIR)
                        stat = sigma_st[:, 2 * g + pair, s * P:(s + 1) * P]
                        nc.tensor.matmul(bank[g][:, cols], stat, mem_hi[:, g, cols], start=True, stop=False)
                        ins = nc.tensor.matmul(bank[g][:, cols], stat, mem_lo[:, g, cols], start=False, stop=True)
                    ins.then_inc(banks_done, 1)

            def comb_transpose(u, first=False):
                pe.wait_ge(comb_done, u + 1)
                if not first:
                    pe.wait_ge(combT_lo_done, u)
                for g in range(K):
                    ins = nc.tensor.transpose(bank[5][:, g * P:(g + 1) * P], combined[:, g], ident[:])
                ins.then_inc(combT_done, 1)

            def wo_product(u, par, first=False, blocks=range(K)):
                if blocks[0] == 0:
                    pe.wait_ge(combT_lo_done, u + 1)
                    if not first:
                        pe.wait_ge(attn_scaled_done, u)
                for g in blocks:
                    ins = mm3(bank[4][:], (combT_hi[par][:, g], combT_lo[par][:, g]),
                              (wo_hi[:, g], wo_lo[:, g]), g == 0, g == K - 1)
                if blocks[-1] == K - 1:
                    ins.then_inc(wo_done, 1)

            pe.wait_ge(ident_ready, 1)
            for k in range(K):
                if k == 1:
                    pe.wait_ge(mods_ready, 1)
                t1(0, k)
            pe.wait_ge(consts_ready, 1)
            pe.wait_ge(norm_in, 80)
            nc.tensor.matmul(bank[5][:, 0:K * NB], ones[:], norm_raw[:].rearrange("p k n -> p (k n)"),
                             start=True, stop=True).then_inc(active_mm, 1)
            pe.wait_ge(wa_hi, 1)
            for g in range(K):
                q_block(0, g, first=True)
            mod_row(GA, x_ring[:, place(2)], bank[4]).then_inc(gates_mm, 1)
            pe.wait_ge(gate_ready, 1)
            mod_row(GB, wmod_sb[:, 0], bank[5]).then_inc(gates_mm, 1)

            def tile(t, first=False, last=False):
                u = 4 * t
                if not first:
                    wo_product(u - 2, 0)
                    comb_transpose(u - 1)
                pe.wait_ge(sigma_done, 4 * t + 4)
                norms(u, 0)
                banks_of(t, 0)
                if first:
                    mod_row(SB, xn2, bank[7]).then_inc(rows_mm, 1)
                if not first:
                    wo_product(u - 1, 1)
                pe.wait_ge(clip_done, u + 1)
                norms(u + 1, 1)
                banks_of(t, 1)
                pe.wait_ge(clip_done, u + 2)
                norms(u + 2, 2)
                if first:
                    pe.wait_ge(gates_ready, 1)
                comb_transpose(u, first=first)
                banks_of(t, 2)
                if not last:
                    pe.wait_ge(clip_done, u + 3)
                    t1(t + 1, 0)
                    if first:
                        pe.wait_ge(rows_done, 1)
                    t1(t + 1, 1)
                if first:
                    pe.wait_ge(wa_lo, 1)
                wo_product(u, 0, first=first, blocks=(0, 1))
                if not last:
                    t1(t + 1, 2)
                    t1(t + 1, 3)
                wo_product(u, 0, blocks=(2, 3))
                comb_transpose(u + 1)
                if last:
                    pe.wait_ge(clip_done, u + 3)
                else:
                    pe.wait_ge(h1_full_done, 4 * (t + 1) + 3)
                norms(u + 3, 3)
                banks_of(t, 3)
                wo_product(u + 1, 1)
                if first:
                    pe.wait_ge(h1_full_done, 8)
                    mod_row(CB, h2_full, bank[7]).then_inc(rows_mm, 1)
                else:
                    pe.wait_ge(clip_done, u + 4)
                    t2(t - 1, 0)
                    if not last:
                        pe.wait_ge(h1_full_done, 4 * (t + 1) + 4)
                    t2(t - 1, 1)
                comb_transpose(u + 2)
                if last:
                    pe.wait_ge(banks_r_done, 16 * NT)
                    gate_or_up(0, 0, 0, 0, 0, first=True)
                else:
                    q_block(t + 1, 0)
                if first:
                    pe.wait_ge(rows_done, 2)
                    pe.wait_ge(clip_done, 4)
                    for i in range(2):
                        for f in range(K):
                            at = (i * K + f) * B
                            ins = nc.tensor.transpose(bank[6][:, at:at + B], mod_rows[:, i, f * P:(f + 1) * P],
                                                      ident[0:B, 0:B])
                    ins.then_inc(mods_mm, 1)
                else:
                    t2(t - 1, 2)
                    t2(t - 1, 3)
                if not last:
                    for g in range(1, K):
                        q_block(t + 1, g)

            def gate_or_up(t2, cc, chunk, j, m, first=False):
                n = 2 * t2 + cc
                hi, lo = (gate_w, up_w)[m][cc]
                if j == 0:
                    w_lo_wait(pe, (chunk, m))
                if not (first and j < 2):
                    pe.wait_ge((silu_done, h_done)[m], 4 * n + j - 1)
                for k in range(K):
                    if cc == 0 and j == 0 and m == 0:
                        pe.wait_ge(h2_lo_done, 4 * t2 + k + 1)
                    ins = mm3(bank[2 * (j % 2) + m][:], (hi[:, k, j], lo[:, k, j]),
                              (h2_hi[:, k], h2_lo[:, k]), k == 0, k == K - 1)
                ins.then_inc((gate_done, up_done)[m], 1)

            def gate_up(t2, cc, chunk):
                for j in range(J):
                    for m in range(2):
                        gate_or_up(t2, cc, chunk, j, m)

            tile(0, first=True)
            with pe.Fori(1, NT - 1) as t:
                tile(t)
            tile(NT - 1, last=True)

            def down(t2, cc, chunk, first=False):
                n = 2 * t2 + cc
                w_lo_wait(pe, (chunk, 2))
                if cc == 0 and first:
                    pe.wait_ge(attn_scaled_done, 4 * NT)
                    pe.wait_ge(h2_full_done, 4 * NT)
                elif cc == 0:
                    pe.wait_ge(y_scaled, 4 * t2)
                for s in range(S):
                    for j in range(J):
                        if s == 0:
                            pe.wait_ge(hs_lo_done, 4 * n + j + 1)
                        cols = slice(s * P, (s + 1) * P)
                        ins = mm3(bank[4 + s][:], (hs_hi[:, j, cols], hs_lo[:, j, cols]),
                                  (down_w[cc][0][:, j], down_w[cc][1][:, j]),
                                  cc == 0 and j == 0, cc == SLOTS - 1 and j == J - 1)
                    ins.then_inc(down_done, 1)

            def tile_b(t2, pass_, prev_pass):
                gate_up(t2, 0, 2 * pass_)
                down(t2 - 1, 1, 2 * prev_pass + 1)
                gate_up(t2, 1, 2 * pass_ + 1)
                down(t2, 0, 2 * pass_)

            wo_product(4 * NT - 2, 0)
            comb_transpose(4 * NT - 1)
            gate_or_up(0, 0, 0, 0, 1, first=True)
            wo_product(4 * NT - 1, 1)
            gate_or_up(0, 0, 0, 1, 0, first=True)
            gate_or_up(0, 0, 0, 1, 1, first=True)
            gate_or_up(0, 0, 0, 2, 0)
            t2(NT - 1, 0)
            t2(NT - 1, 1)
            gate_or_up(0, 0, 0, 2, 1)
            t2(NT - 1, 2)
            t2(NT - 1, 3)
            gate_or_up(0, 0, 0, 3, 0)
            gate_or_up(0, 0, 0, 3, 1)
            gate_up(0, 1, 1)
            down(0, 0, 0, first=True)
            with pe.Fori(1, NT) as t2_:
                tile_b(t2_, 0, 0)
            tile_b(NT, 1, 0)
            with pe.Fori(NT + 1, NT2) as t2_:
                tile_b(t2_, 1, 1)
            down(NT2 - 1, 1, CHUNKS - 1)


_INS = ["x", "wqT", "woT", "bank_w", "mem_hd", "norm_hd", "w_gate", "w_up", "w_down", "cT", "wmod"]


def kernel(**inputs):
    import numpy as _np
    import concourse.bacc as _bacc
    from concourse import mybir as _mybir
    from concourse.bass_utils import run_bass_kernel_spmd as _run

    a = {n: _np.asarray(v) for n, v in inputs.items()}
    x = a["L0_attn_hidden_states"]
    b, s, d = x.shape
    mem, norm = a["L0_attn_memories"], a["L0_attn_memory_norms"]
    nb, h, dh, _ = mem.shape
    laid = {
        "x": x.reshape(b * s, d),
        "wqT": a["L0_attn_Wq"].T,
        "woT": a["L0_attn_Wo"].T,
        "bank_w": a["L0_attn_bank_weights"],
        "mem_hd": mem.transpose(1, 2, 0, 3).reshape(h * dh, nb, dh),
        "norm_hd": norm.transpose(1, 2, 0).reshape(h * dh, nb),
        "w_gate": a["L0_ffn_w_gate"],
        "w_up": a["L0_ffn_w_up"],
        "w_down": a["L0_ffn_w_down"],
        "cT": a["L0_c"].T,
        "wmod": a["L0_wmod"],
    }
    nc = _bacc.Bacc("TRN2", target_bir_lowering=False, num_devices=1)
    arrays, args = {}, []
    for name in _INS:
        v = _np.ascontiguousarray(laid[name])
        arrays[f"in_{name}_dram"] = v
        args.append(nc.dram_tensor(f"in_{name}_dram", v.shape, _mybir.dt.from_np(v.dtype), kind="ExternalInput").ap())
    out = nc.dram_tensor("out_dram", (b * s, d), _mybir.dt.float32, kind="ExternalOutput").ap()
    adaln_kernel(nc, *args, out)
    r = _run(nc, [arrays], core_ids=[0])
    return r.results[0]["out_dram"].reshape(b, s, d)
```
